# Optimizing a Trainium2 kernel written in Bass

```python
import numpy as np
import jax
import jax.numpy as jnp

def _softmax(x, axis=-1):
    return jax.nn.softmax(x, axis=axis)

def _gelu(x):
    return jax.nn.gelu(x, approximate=True)

def _silu(x):
    return jax.nn.silu(x)

def _sigmoid(x):
    return jax.nn.sigmoid(x)

def _layernorm(x, axis=-1, eps=1e-05):
    m = jnp.mean(x, axis=axis, keepdims=True)
    v = jnp.var(x, axis=axis, keepdims=True)
    return (x - m) / jnp.sqrt(v + eps)

def _scatter_add(tgt, idx, src, axis=0):
    return tgt.at[idx].add(src)

def _segment_sum(src, seg, n):
    return jax.ops.segment_sum(src, seg, n)
kernel_name = 'mk_seq_preln_d1_jaxref_r4_85e362'

def setup_inputs(seed: int=0):
    np.random.seed(seed)
    _w = jnp.asarray

    def _L0_attn_setup():
        import jax, jax.numpy as jnp
        import numpy as np
        B, S, D, H = (2, 512, 256, 16)
        HD = D // H
        key = jax.random.key(seed)
        ks = jax.random.split(key, 5)
        return {'x': jax.random.normal(ks[0], (B, S, D), dtype=jnp.float32), 'qkv_w': jax.random.normal(ks[1], (3 * D, D), dtype=jnp.float32) * (1.0 / np.sqrt(D)), 'qkv_b': jax.random.normal(ks[2], (3 * D,), dtype=jnp.float32) * 0.02, 'proj_w': jax.random.normal(ks[3], (D, D), dtype=jnp.float32) * (1.0 / np.sqrt(D)), 'proj_b': jax.random.normal(ks[4], (D,), dtype=jnp.float32) * 0.02}
    _L0_attn_in = _L0_attn_setup()

    def _L0_ffn_setup():
        import jax, jax.numpy as jnp
        import numpy as np
        FP8_MAX = 448.0
        key = jax.random.key(seed)
        k_x, k_w, k_b = jax.random.split(key, 3)
        B, S, IN, OUT = (4, 2048, 256, 256)
        x = jax.random.normal(k_x, (B, S, IN), dtype=jnp.float32)
        w_fp32 = jax.random.normal(k_w, (OUT, IN), dtype=jnp.float32)
        weight_fp8 = w_fp32.astype(jnp.float8_e4m3fn).astype(jnp.float32)
        bias = jax.random.normal(k_b, (OUT,), dtype=jnp.float32)
        input_scale = jnp.ones((1,), dtype=jnp.float32)
        weight_scale = jnp.ones((1,), dtype=jnp.float32)
        return {'x': x, 'weight_fp8': weight_fp8, 'bias': bias, 'input_scale': input_scale, 'weight_scale': weight_scale}
    _L0_ffn_in = _L0_ffn_setup()
    _d = {'L0_attn_x': _L0_attn_in['x'], 'L0_attn_qkv_w': _L0_attn_in['qkv_w'], 'L0_attn_qkv_b': _L0_attn_in['qkv_b'], 'L0_attn_proj_w': _L0_attn_in['proj_w'], 'L0_attn_proj_b': _L0_attn_in['proj_b'], 'L0_ffn_weight_fp8': _L0_ffn_in['weight_fp8'], 'L0_ffn_bias': _L0_ffn_in['bias'], 'L0_ffn_input_scale': _L0_ffn_in['input_scale'], 'L0_ffn_weight_scale': _L0_ffn_in['weight_scale']}
    _x0 = _d['L0_attn_x']
    _d['L0_attn_x'] = jax.random.normal(jax.random.fold_in(jax.random.key(seed), 1), (16, 512, 256), dtype=_x0.dtype)
    del _x0
    return _d

def reference(L0_attn_x, L0_attn_qkv_w, L0_attn_qkv_b, L0_attn_proj_w, L0_attn_proj_b, L0_ffn_weight_fp8, L0_ffn_bias, L0_ffn_input_scale, L0_ffn_weight_scale):

    def _L0_attn_ref(x, qkv_w, qkv_b, proj_w, proj_b):
        import jax, jax.numpy as jnp
        import numpy as np
        B, S, D, H = (2, 512, 256, 16)
        HD = D // H
        b, s, d = x.shape
        qkv = jnp.einsum('bsd,ed->bse', x, qkv_w) + qkv_b
        qkv = qkv.reshape(b, s, 3, H, HD)
        q = jnp.transpose(qkv[:, :, 0], (0, 2, 1, 3))
        k = jnp.transpose(qkv[:, :, 1], (0, 2, 1, 3))
        v = jnp.transpose(qkv[:, :, 2], (0, 2, 1, 3))
        scale = 1.0 / jnp.sqrt(jnp.asarray(HD, dtype=x.dtype))
        scores = jnp.einsum('bhqe,bhke->bhqk', q, k) * scale
        attn = jax.nn.softmax(scores, axis=-1)
        out = jnp.einsum('bhqk,bhke->bhqe', attn, v)
        out = jnp.transpose(out, (0, 2, 1, 3)).reshape(b, s, d)
        out = jnp.einsum('bsd,ed->bse', out, proj_w) + proj_b
        return out

    def _L0_ffn_ref(x, weight_fp8, bias, input_scale, weight_scale):
        import jax, jax.numpy as jnp
        import numpy as np
        FP8_MAX = 448.0
        x_q = jnp.clip(x / input_scale, -FP8_MAX, FP8_MAX)
        x_dq = x_q.astype(jnp.float8_e4m3fn).astype(x.dtype) * input_scale
        w_dq = weight_fp8 * weight_scale
        out = jnp.einsum('bsi,oi->bso', x_dq, w_dq) + bias
        return out
    x = L0_attn_x
    x = x + _L0_attn_ref(_layernorm(x, axis=-1), L0_attn_qkv_w, L0_attn_qkv_b, L0_attn_proj_w, L0_attn_proj_b)
    x = x + _L0_ffn_ref(_layernorm(x, axis=-1), L0_ffn_weight_fp8, L0_ffn_bias, L0_ffn_input_scale, L0_ffn_weight_scale)
    return x

_drawn_inputs = setup_inputs


def setup_inputs(seed=0):
    import zlib

    import numpy as np

    out = dict(_drawn_inputs(seed))
    spreads = {}
    factors = {}
    for name, (base, spread) in spreads.items():
        noise = np.random.default_rng([zlib.crc32(name.encode()), seed]).standard_normal(out[name].shape)
        drawn = base * np.exp(spread * noise) if base else spread * noise
        out[name] = jnp.asarray(drawn.astype(out[name].dtype))
    for name, factor in factors.items():
        out[name] = (out[name] * factor).astype(out[name].dtype)
    return out
```

```python
from contextlib import ExitStack

import concourse.bass as bass
from concourse import mybir

F32 = mybir.dt.float32
BF16 = mybir.dt.bfloat16
U32 = mybir.dt.uint32
ALU = mybir.AluOpType
ACT = mybir.ActivationFunctionType
AX_X = mybir.AxisListType.X

P = 128
B, S, D, H = 16, 512, 256, 16
HD = D // H
SCALE = float(HD) ** -0.5
EPS = 1e-5
NJ = S // P
NC = D // P
HT = P // HD
NT = H // HT
Q_PARTS = [0, 0, 1, 0, 2, 1]
K_PARTS = [0, 1, 0, 2, 0, 1]
KR = HD * len(Q_PARTS)
KM = KR + 3
VW = 32
FP8_MAX = 448.0
FP8_MIN_NORMAL = 2.0 ** -6
FP8_ROUND = 1.5 * 2.0 ** 20
EXPONENT = 0x7F800000

STEPS = 32
UNITS = STEPS // 4
NSLOT = B + 3
LOOP_FROM, LOOP_TO = 4, 14


def block_kernel(nc, x, qkv_wT, qk_bT, v_bT, proj_wT, proj_b, lin_wT, lin_b, in_scale, w_scale, eye, out):
    x_d = x.rearrange("b (p j) d -> b p j d", j=NJ)
    out_d = out.rearrange("b (p j) d -> b p j d", j=NJ)

    with ExitStack() as ctx:
        def sb(name, shape, dt=F32):
            return ctx.enter_context(nc.sbuf_tensor(name, shape, dt))

        def ps(name, shape):
            return ctx.enter_context(nc.psum_tensor(name, shape, F32))

        def sem(name):
            return ctx.enter_context(nc.semaphore(name))

        wqkv = sb("wqkv", [P, NC, 3 * D])
        wproj = sb("wproj", [P, NC, D])
        wlin = sb("wlin", [P, NC, D])
        wlin_rest = sb("wlin_rest", [P, NC, D])
        wlin_p = sb("wlin_p", [P, 3, NC, D], BF16)
        b_qk = sb("b_qk", [P, 2 * NT])
        b_v = sb("b_v", [P, NT])
        b_v_rep = sb("b_v_rep", [P, NT, P])
        b_proj = sb("b_proj", [P, D])
        b_lin = sb("b_lin", [P, D])
        s_in = sb("s_in", [P, 1])
        s_w = sb("s_w", [P, 1])
        s_inv = sb("s_inv", [P, 1])
        ident = sb("ident", [P, P])
        ident_b = sb("ident_b", [P, P], BF16)
        half_neg = sb("half_neg", [P, NJ])
        xin = [sb(f"xin{i}", [P, NJ, D]) for i in range(2)]
        st1 = sb("st1", [P, NJ, 6])
        mv1 = sb("mv1", [P, NJ, 2])
        nm1 = sb("nm1", [P, NJ])
        ve1 = sb("ve1", [P, NJ])
        rs1 = sb("rs1", [P, NJ])
        xn = sb("xn", [P, NJ, D])
        xnT = sb("xnT", [P, NC, S])
        parts = sb("parts", [P, 2 * NT, 3, S], BF16)
        whole = sb("whole", [P, 2, S])
        rest = sb("rest", [P, 2, S])
        qs = [sb(f"qs{i}", [P, H, S], BF16) for i in range(2)]
        ks = [sb(f"ks{i}", [P, H, S], BF16) for i in range(2)]
        vt = [sb(f"vt{i}", [P, NJ, H, VW]) for i in range(2)]
        mx = sb("mx", [P, NT, HT * NJ])
        nmax = sb("nmax", [HT * NJ, NT, 3, P], BF16)
        nmax_r = sb("nmax_r", [HT * NJ, P])
        pt = [sb(f"pt{i}", [P, 4, 2, S]) for i in range(2)]
        ot = sb("ot", [P, S // 32, 32])
        rden = sb("rden", [P, S // 32])
        on = sb("on", [P, S // 32, 32])
        oT = sb("oT", [P, NT, S])
        xres = sb("xres", [P, NJ, D])
        h = sb("h", [P, NJ, D])
        hb = sb("hb", [P, NJ, D])
        st2 = sb("st2", [P, NJ, 6])
        mv2 = sb("mv2", [P, NJ, 2])
        nm2 = sb("nm2", [P, NJ])
        ve2 = sb("ve2", [P, NJ])
        rs2 = sb("rs2", [P, NJ])
        hn = sb("hn", [P, NJ, D])
        cr = sb("cr", [P, NJ, D])
        hq = sb("hq", [P, NJ, D], BF16)
        hqT = sb("hqT", [P, NC, S], BF16)
        y = sb("y", [P, NJ, D])

        ps_t = ps("ps_t", [P, 2, S])
        ps_s = ps("ps_s", [P, 2, 2, S])
        ps_o = ps("ps_o", [P, S])
        ps_m = ps("ps_m", [P, S])

        consts = sem("consts")
        const_v = sem("const_v")
        bias_done = sem("bias_done")
        ones = sem("ones")
        x_in = [sem(f"x_in{i}") for i in range(2)]
        xr_in = sem("xr_in")
        stacked = [[sem(f"stacked{t}{i}") for i in range(2)] for t in range(NT)]
        rows_in = [sem(f"rows_in{t}") for t in range(NT)]
        stored = sem("stored")
        met = sem("met")
        xt_done = sem("xt_done")
        qk_done = sem("qk_done")
        v_done = sem("v_done")
        s_done = sem("s_done")
        mt_done = sem("mt_done")
        st_done = sem("st_done")
        pv_done = sem("pv_done")
        proj_done = sem("proj_done")
        xq_done = sem("xq_done")
        lin_done = sem("lin_done")
        xnT_ready = sem("xnT_ready")
        part1 = sem("part1")
        whole_ready = sem("whole_ready")
        v_ready = sem("v_ready")
        exp_done = sem("exp_done")
        hqT_ready = sem("hqT_ready")
        ln1_sums = sem("ln1_sums")
        ln1_mv = sem("ln1_mv")
        ln1_ready = sem("ln1_ready")
        ln2_sums = sem("ln2_sums")
        ln2_mv = sem("ln2_mv")
        ln2_ready = sem("ln2_ready")
        max_done = sem("max_done")
        nmax_split = sem("nmax_split")
        ot_ready = sem("ot_ready")
        rden_ready = sem("rden_ready")
        on_ready = sem("on_ready")
        oT_ready = sem("oT_ready")
        h_ready = sem("h_ready")
        clipped = sem("clipped")
        pow2 = sem("pow2")
        round_c = sem("round_c")
        y_ready = sem("y_ready")
        half_set = sem("half_set")
        rs1_ready = sem("rs1_ready")
        xn_ready = sem("xn_ready")
        rest_ready = sem("rest_ready")
        part2 = sem("part2")
        part3 = sem("part3")
        res_ready = sem("res_ready")
        rs2_pow = sem("rs2_pow")
        rs2_ready = sem("rs2_ready")
        hn_ready = sem("hn_ready")
        hb_ready = sem("hb_ready")
        sum_c = sem("sum_c")
        hq_ready = sem("hq_ready")

        def past(count):
            return not isinstance(count, int) or count > 0

        def run_slots(eng, slot):
            def present(u):
                return lambda behind: 0 <= u - behind < B
            for u in range(LOOP_FROM):
                slot(u, u % 2, present(u))
            with eng.Fori(0, (LOOP_TO - LOOP_FROM) // 2) as i:
                for half in range(2):
                    slot(i * 2 + (LOOP_FROM + half), half, lambda behind: True)
            for u in range(LOOP_TO, NSLOT):
                slot(u, u % 2, present(u))

        block = ctx.enter_context(nc.Block())

        @block.sync
        def _(sp):
            sp.dma_start(xin[0][:], x_d[0]).then_inc(x_in[0], 16)
            for dst, src in ((wqkv[:], qkv_wT.rearrange("(c p) e -> p c e", p=P)),
                             (ident[:], eye), (b_qk[:], qk_bT),
                             (b_v[:], v_bT),
                             (wproj[:], proj_wT.rearrange("(c p) e -> p c e", p=P)),
                             (wlin[:], lin_wT.rearrange("(c p) e -> p c e", p=P)),
                             (b_proj[:], proj_b.partition_broadcast(P)),
                             (b_lin[:], lin_b.partition_broadcast(P)),
                             (s_in[:], in_scale.partition_broadcast(P)),
                             (s_w[:], w_scale.partition_broadcast(P))):
                sp.dma_start(dst, src).then_inc(consts, 16)

            def settled():
                sp.sem_inc(met, 1)

            def load(b, par):
                if past(b - 1):
                    sp.wait_ge(xn_ready, b - 1)
                settled()
                sp.dma_start(xin[par][:], x_d[bass.ds(b, 1)].rearrange("a p j d -> (a p) j d")).then_inc(x_in[par], 16)

            def reload(b, par):
                if past(b):
                    sp.wait_ge(h_ready, 2 * b)
                settled()
                sp.dma_start(xres[:], x_d[bass.ds(b, 1)].rearrange("a p j d -> (a p) j d")).then_inc(xr_in, 16)

            def stack(b, par, t):
                sp.wait_ge(part3, 4 * b + 2 * t + 2)
                settled()
                if past(2 * STEPS * (b - 2) + (t + 1) * STEPS):
                    sp.wait_ge(st_done, 2 * STEPS * (b - 2) + (t + 1) * STEPS)
                settled()
                for r, (pq, pk) in enumerate(zip(Q_PARTS, K_PARTS)):
                    rows = slice(HD * r, HD * (r + 1))
                    for dst, src in ((qs, parts[:, 2 * t, pq, :]), (ks, parts[:, 2 * t + 1, pk, :])):
                        sp.dma_start(dst[par][rows, HT * t:HT * (t + 1), :], src).then_inc(stacked[t][par], 16)

            def rows(b, par, t):
                sp.wait_ge(nmax_split, 8 * b + 4 * t + 4)
                settled()
                for i in range(3):
                    sp.dma_start(qs[par][KR + i:KR + i + 1, HT * t:HT * (t + 1), :],
                                 nmax[:, t, i, :]).then_inc(rows_in[t], 16)

            def store(b, par):
                sp.wait_ge(y_ready, 2 * b + 2)
                settled()
                sp.dma_start(out_d[bass.ds(b, 1)].rearrange("a p j d -> (a p) j d"), y[:]).then_inc(stored, 16)

            def slot(u, par, present):
                if present(-1):
                    load(u + 1, 1 - par)
                if present(2):
                    rows(u - 2, par, 1)
                    reload(u - 2, par)
                if present(0):
                    stack(u, par, 0)
                if present(1):
                    rows(u - 1, 1 - par, 0)
                if present(3):
                    store(u - 3, 1 - par)
                if present(0):
                    stack(u, par, 1)

            run_slots(sp, slot)
            sp.wait_ge(stored, 16 * B)

        @block.tensor
        def _(pe):
            bank_user = [None, 0, 0]

            def take_bank(u, name, n, behind):
                last, m, b = bank_user[0], bank_user[1], u - bank_user[2]
                if last in ("transpose_x", "project_qk", "project_v"):
                    reader, value = {"transpose_x": (xnT_ready, 2 * b), "project_qk": (whole_ready, 4 * b),
                                     "project_v": (v_ready, 2 * b)}[last]
                    pe.wait_ge(reader, value + m + 1)
                elif last == "transpose_max":
                    pe.wait_ge(nmax_split, 8 * b + 4 * m + 2)
                elif last == "project_out":
                    pe.wait_ge(h_ready, 2 * b + m + 1)
                elif last == "transpose_hq":
                    pe.wait_ge(hqT_ready, b + 1)
                elif last == "linear":
                    pe.wait_ge(y_ready, 2 * b + m + 1)
                bank_user[:] = [name, n, behind]

            def transpose_x(u, c):
                take_bank(u, "transpose_x", c, 0)
                pe.wait_ge(xn_ready, u + 1)
                for j in range(NJ):
                    last = nc.tensor.transpose(ps_m[:, j * P:(j + 1) * P], xn[:, j, c * P:(c + 1) * P], ident[:])
                last.then_inc(xt_done, 1)

            def project_qk(u, n):
                take_bank(u, "project_qk", n, 0)
                if n == 0:
                    pe.wait_ge(xnT_ready, 2 * u + 2)
                first = (n % 2) * D + (n // 2) * P
                for c in range(NC):
                    last = nc.tensor.matmul(ps_m[:], wqkv[:, c, first:first + P], xnT[:, c, :],
                                            start=(c == 0), stop=(c == NC - 1))
                last.then_inc(qk_done, 1)

            def project_v(u, half):
                take_bank(u, "project_v", half, 1)
                for j in range(2):
                    tok = slice((2 * half + j) * P, (2 * half + j + 1) * P)
                    for c in range(NC):
                        last = nc.tensor.matmul(ps_m[:, j * D:(j + 1) * D], xnT[:, c, tok], wqkv[:, c, 2 * D:3 * D],
                                                start=(c == 0), stop=(c == NC - 1))
                last.then_inc(v_done, 1)

            def transpose_max(u, t, behind):
                take_bank(u, "transpose_max", t, behind)
                pe.wait_ge(max_done, STEPS * (u - behind) + (t + 1) * STEPS // 2)
                nc.tensor.transpose(ps_m[0:HT * NJ, 0:P], mx[:, t, :], ident[:]).then_inc(mt_done, 1)

            def project_out(u, half):
                take_bank(u, "project_out", half, 3)
                if half == 0:
                    pe.wait_ge(oT_ready, NT * (u - 3) + NT)
                for j in range(2):
                    tok = slice((2 * half + j) * P, (2 * half + j + 1) * P)
                    for t in range(NT):
                        last = nc.tensor.matmul(ps_m[:, j * D:(j + 1) * D], oT[:, t, tok], wproj[:, t, :],
                                                start=(t == 0), stop=(t == NT - 1))
                last.then_inc(proj_done, 1)

            def transpose_hq(u):
                take_bank(u, "transpose_hq", 0, 3)
                pe.wait_ge(hq_ready, u - 3 + 1)
                psb = ps_m[:].bitcast(BF16)
                for c in range(NC):
                    for j in range(NJ):
                        last = nc.tensor.transpose(psb[:, c * S + j * P:c * S + (j + 1) * P],
                                                   hq[:, j, c * P:(c + 1) * P], ident_b[:])
                last.then_inc(xq_done, 1)

            def linear(u, half):
                take_bank(u, "linear", half, 3)
                if half == 0:
                    pe.wait_ge(hqT_ready, u - 3 + 1)
                for j in range(2):
                    tok = slice((2 * half + j) * P, (2 * half + j + 1) * P)
                    for c in range(NC):
                        for part in range(3):
                            last = nc.tensor.matmul(ps_m[:, j * D:(j + 1) * D], hqT[:, c, tok], wlin_p[:, part, c, :],
                                                    start=(c == 0 and part == 0),
                                                    stop=(c == NC - 1 and part == 2))
                last.then_inc(lin_done, 1)

            def scores_t(b, par, s, a):
                n, i = s // 4, s % 4
                t, odd, kp = n // 4, n // 2 % 2, n % 2
                head = HT * t + 2 * i + odd
                if s in (0, STEPS // 2) and a == 0:
                    pe.wait_ge(rows_in[t], 48 * b + 48)
                if past(2 * STEPS * b + 2 * s + a - 1):
                    pe.wait_ge(exp_done, 2 * STEPS * b + 2 * s + a - 1)
                keys = slice((2 * kp + a) * P, (2 * kp + a + 1) * P)
                nc.tensor.matmul(ps_t[:, a, :], ks[par][0:KM, head, keys], qs[par][0:KM, head, :],
                                 start=True, stop=True).then_inc(st_done, 1)

            def scores(b, par, s, a):
                head = s // 2
                if s in (0, STEPS // 2) and a == 0:
                    t = s // (STEPS // 2)
                    pe.wait_ge(stacked[t][par], 96 * (b - par) + 192)
                if a == 0 and past(STEPS * b + s - 1):
                    pe.wait_ge(max_done, STEPS * b + s - 1)
                queries = slice((2 * (s % 2) + a) * P, (2 * (s % 2) + a + 1) * P)
                last = nc.tensor.matmul(ps_s[:, s % 2, a, :], qs[par][0:KR, head, queries],
                                        ks[par][0:KR, head, :], start=True, stop=True)
                if a == 1:
                    last.then_inc(s_done, 1)

            def values(b, par, n, a):
                t, odd, kp = n // 4, n // 2 % 2, n % 2
                if a == 0:
                    if n == 0:
                        pe.wait_ge(v_ready, 2 * b + 2)
                    pe.wait_ge(exp_done, 2 * (STEPS * b + 4 * n + 4))
                    if kp == 0:
                        if past(4 * b + n // 2):
                            pe.wait_ge(ot_ready, 4 * b + n // 2)
                for i in range(4):
                    head = HT * t + 2 * i + odd
                    last = nc.tensor.matmul(ps_o[32 * i:32 * i + VW, :], vt[par][:, 2 * kp + a, head, :],
                                            pt[n % 2][:, i, a, :], start=(kp == 0 and a == 0),
                                            stop=(kp == 1 and a == 1))
                if a == 1:
                    last.then_inc(pv_done, 1)

            def slot(u, par, present):
                bank_user[2] += 1
                for s in range(STEPS):
                    if present(2):
                        scores_t(u - 2, par, s, 0)
                    if present(1):
                        scores(u - 1, 1 - par, s, 0)
                    if s == 2 and present(2):
                        transpose_max(u, 1, 2)
                    if s in (4, 6) and present(1):
                        project_v(u, s // 2 - 2)
                    if s in (8, 10) and present(3):
                        project_out(u, s // 2 - 4)
                    if s in (12, 14) and present(0):
                        transpose_x(u, s // 2 - 6)
                    if s in (16, 18) and present(0):
                        project_qk(u, s // 2 - 8)
                    if s == 20 and present(1):
                        transpose_max(u, 0, 1)
                    if s in (22, 24) and present(0):
                        project_qk(u, s // 2 - 9)
                    if s == 26 and present(3):
                        transpose_hq(u)
                    if s in (28, 30) and present(3):
                        linear(u, s // 2 - 14)
                    if s % 2:
                        n = s // 4 - 1
                        if n >= 0 and present(2):
                            values(u - 2, par, n, s // 2 % 2)
                        if n < 0 and present(3):
                            values(u - 3, 1 - par, UNITS - 1, s // 2 % 2)
                    if present(2):
                        scores_t(u - 2, par, s, 1)
                    if present(1):
                        scores(u - 1, 1 - par, s, 1)

            pe.wait_ge(consts, 160)
            pe.wait_ge(const_v, 7)
            for t in range(NT):
                last = nc.tensor.matmul(ps_m[:, 0:D], b_v_rep[:, t, :], wproj[:, t, :],
                                        start=(t == 0), stop=(t == NT - 1))
            last.then_inc(bias_done, 1)
            pe.wait_ge(const_v, 8)
            run_slots(pe, slot)

        @block.scalar
        def _(act):
            def exps(b, s, a):
                n, i = s // 4, s % 4
                if i == 0 and a == 0 and past(UNITS * b + n - 1):
                    act.wait_ge(pv_done, UNITS * b + n - 1)
                act.wait_ge(st_done, 2 * (STEPS * b + s) + a + 1)
                nc.scalar.activation(pt[n % 2][:, i, a, :], ps_t[:, a, :], ACT.Exp, scale=SCALE).then_inc(exp_done, 1)

            def copy_v(b, par, half):
                act.wait_ge(v_done, 2 * b + half + 1)
                if past(UNITS * (b - 1)):
                    act.wait_ge(pv_done, UNITS * (b - 1))
                nc.scalar.copy(vt[par][:, 2 * half:2 * half + 2, :, 0:HD],
                               ps_m[:].rearrange("p (j h e) -> p j h e", j=2, h=H)).then_inc(v_ready, 1)

            def copy_xnT(b, c):
                act.wait_ge(xt_done, 2 * b + c + 1)
                if past(b):
                    act.wait_ge(v_done, 2 * b)
                nc.scalar.copy(xnT[:, c, :], ps_m[:]).then_inc(xnT_ready, 1)

            def copy_qk(b, par, n):
                t, bias = n // 2, b_qk[:, (n % 2) * NT + n // 2:(n % 2) * NT + n // 2 + 1]
                act.wait_ge(qk_done, 4 * b + n + 1)
                if past(b):
                    act.wait_ge(stacked[t][1 - par], 96 * (b - 2 + par) + 192)
                nc.scalar.activation(parts[:, n, 0, :], ps_m[:], ACT.Identity, bias=bias).then_inc(part1, 1)
                if past(4 * b + n - 1):
                    act.wait_ge(rest_ready, 4 * b + n - 1)
                nc.scalar.activation(whole[:, n % 2, :], ps_m[:], ACT.Identity, bias=bias).then_inc(whole_ready, 1)

            def copy_hqT(b):
                act.wait_ge(xq_done, b + 1)
                if past(b):
                    act.wait_ge(lin_done, 2 * b)
                nc.scalar.copy(hqT[:].rearrange("p c n -> p (c n)"), ps_m[:].bitcast(BF16)).then_inc(hqT_ready, 1)

            def slot(u, par, present):
                for s in range(STEPS):
                    if present(2):
                        exps(u - 2, s, 0)
                    if s in (5, 7) and present(1):
                        copy_v(u - 1, 1 - par, s // 2 - 2)
                    if s in (13, 15) and present(0):
                        copy_xnT(u, s // 2 - 6)
                    if s in (17, 19) and present(0):
                        copy_qk(u, par, s // 2 - 8)
                    if s in (23, 25) and present(0):
                        copy_qk(u, par, s // 2 - 9)
                    if s == 27 and present(3):
                        copy_hqT(u - 3)
                    if present(2):
                        exps(u - 2, s, 1)

            act.wait_ge(consts, 160)
            run_slots(act, slot)

        @block.vector
        def _(dve):
            dve.memset(ks[0][96:KM, :, :], 1.0).then_inc(ones, 1)
            dve.memset(ks[1][96:KM, :, :], 1.0).then_inc(ones, 1)
            dve.memset(vt[0][:], 1.0).then_inc(ones, 1)
            dve.memset(vt[1][:], 1.0).then_inc(ones, 1)
            dve.memset(half_neg[:], -0.5).then_inc(half_set, 1)
            dve.wait_ge(ones, 4)
            dve.wait_ge(consts, 160)
            dve.tensor_copy(ident_b[:], ident[:]).then_inc(const_v, 1)
            dve.reciprocal(s_inv[:], s_in[:]).then_inc(const_v, 1)
            dve.tensor_scalar(wlin_rest[:], wlin[:], s_w[:, 0:1], None, ALU.mult).then_inc(const_v, 1)
            dve.wait_ge(const_v, 3)
            dve.tensor_copy(wlin_p[:, 0], wlin_rest[:]).then_inc(const_v, 1)
            dve.wait_ge(const_v, 4)
            dve.tensor_tensor(wlin[:], wlin_rest[:], wlin_p[:, 0], ALU.subtract).then_inc(const_v, 1)
            dve.wait_ge(const_v, 5)
            dve.tensor_copy(wlin_p[:, 1], wlin[:]).then_inc(ones, 1)
            dve.wait_ge(ones, 5)
            dve.tensor_tensor(wlin_p[:, 2], wlin[:], wlin_p[:, 1], ALU.subtract).then_inc(const_v, 1)
            dve.tensor_copy(b_v_rep[:], b_v[:].unsqueeze(2).to_broadcast([P, NT, P])).then_inc(const_v, 1)
            dve.wait_ge(bias_done, 1)
            dve.tensor_tensor(b_proj[:], ps_m[:, 0:D], b_proj[:], ALU.add).then_inc(const_v, 1)

            def maxima(b, s):
                t = s // (STEPS // 2)
                if s in (0, STEPS // 2) and past(NT * (b - 1) + t + 1):
                    dve.wait_ge(mt_done, NT * (b - 1) + t + 1)
                dve.wait_ge(s_done, STEPS * b + s + 1)
                col = 2 * (s % (STEPS // 2))
                dve.tensor_reduce(mx[:, t, col:col + 2], ps_s[:, s % 2, :, :], AX_X, ALU.max).then_inc(max_done, 1)

            def ln1_sum(b, par, j):
                if j == 0:
                    dve.wait_ge(x_in[par], 8 * (b - par) + 16)
                    if past(b):
                        dve.wait_ge(xn_ready, b)
                dve.bn_stats(st1[:, j, :], xin[par][:, j, :]).then_inc(ln1_sums, 1)

            def ln1_finish(b):
                dve.wait_ge(ln1_sums, NJ * b + NJ)
                dve.sem_inc(met, 1)
                for j in range(NJ):
                    last = dve.bn_aggr(mv1[:, j, :], st1[:, j, :])
                last.then_inc(ln1_mv, 1)
                dve.wait_ge(ln1_mv, b + 1)
                dve.tensor_scalar(nm1[:], mv1[:, :, 0], -1.0, None, ALU.mult).then_inc(ln1_ready, 1)
                dve.tensor_scalar(ve1[:], mv1[:, :, 1], EPS, None, ALU.add).then_inc(ln1_ready, 1)

            def ln2_sum(b, j):
                if j == 0 and past(b):
                    dve.wait_ge(hn_ready, b)
                if j % 2 == 0:
                    dve.wait_ge(h_ready, 2 * b + j // 2 + 1)
                    dve.sem_inc(met, 1)
                dve.bn_stats(st2[:, j, :], h[:, j, :]).then_inc(ln2_sums, 1)

            def ln2_finish(b):
                dve.wait_ge(ln2_sums, NJ * b + NJ)
                dve.sem_inc(met, 1)
                for j in range(NJ):
                    last = dve.bn_aggr(mv2[:, j, :], st2[:, j, :])
                last.then_inc(ln2_mv, 1)
                dve.wait_ge(ln2_mv, b + 1)
                dve.tensor_scalar(nm2[:], mv2[:, :, 0], -1.0, None, ALU.mult).then_inc(ln2_ready, 1)
                dve.tensor_scalar(ve2[:], mv2[:, :, 1], EPS, None, ALU.add).then_inc(ln2_ready, 1)

            def split_max(b, t):
                dve.wait_ge(mt_done, NT * b + t + 1)
                if past(b):
                    dve.wait_ge(rows_in[t], 48 * b)
                mT = ps_m[0:HT * NJ, 0:P]
                dve.tensor_scalar(nmax[:, t, 0, :], mT, -1.0, None, ALU.mult).then_inc(nmax_split, 1)
                dve.wait_ge(nmax_split, 8 * b + 4 * t + 1)
                dve.scalar_tensor_tensor(out=nmax_r[:], in0=mT, scalar=-1.0, in1=nmax[:, t, 0, :],
                                         op0=ALU.mult, op1=ALU.subtract).then_inc(nmax_split, 1)
                dve.wait_ge(nmax_split, 8 * b + 4 * t + 2)
                dve.tensor_copy(nmax[:, t, 1, :], nmax_r[:]).then_inc(nmax_split, 1)
                dve.wait_ge(nmax_split, 8 * b + 4 * t + 3)
                dve.tensor_tensor(nmax[:, t, 2, :], nmax_r[:], nmax[:, t, 1, :], ALU.subtract).then_inc(nmax_split, 1)

            def out_blocks(b, g):
                dve.wait_ge(pv_done, UNITS * b + 2 * g + 2)
                if past(4 * b + g):
                    dve.wait_ge(on_ready, 4 * b + g)
                dve.transpose(ot[:].rearrange("p a c -> p (a c)"), ps_o[:]).then_inc(ot_ready, 1)

            def out_divide(b, g):
                dve.wait_ge(ot_ready, 4 * b + g + 1)
                dve.reciprocal(rden[:], ot[:, :, HD]).then_inc(rden_ready, 1)
                dve.wait_ge(rden_ready, 4 * b + g + 1)
                if g % 2 == 0 and past(NT * b + g // 2):
                    dve.wait_ge(oT_ready, NT * b + g // 2)
                half = slice(HD * (g % 2), HD * (g % 2) + HD)
                dve.tensor_tensor(on[:, :, half], ot[:, :, 0:HD], rden[:].unsqueeze(2).to_broadcast([P, S // 32, HD]),
                                  ALU.mult).then_inc(on_ready, 1)

            def out_back(b, t):
                dve.wait_ge(on_ready, 4 * b + 2 * t + 2)
                if past(b):
                    dve.wait_ge(proj_done, 2 * b)
                dve.transpose(oT[:, t, :], on[:].rearrange("p a c -> p (a c)")).then_inc(oT_ready, 1)

            def add_residual(b, half):
                dve.wait_ge(proj_done, 2 * b + half + 1)
                if half == 0:
                    dve.wait_ge(res_ready, b + 1)
                    if past(b):
                        dve.wait_ge(hb_ready, b)
                tok = slice(2 * half, 2 * half + 2)
                dve.tensor_tensor(h[:, tok, :].rearrange("p j d -> p (j d)"), ps_m[:],
                                  xres[:, tok, :].rearrange("p j d -> p (j d)"), ALU.add).then_inc(h_ready, 1)

            def clip(b):
                dve.wait_ge(hn_ready, b + 1)
                dve.tensor_scalar(hn[:], hn[:], FP8_MAX, -FP8_MAX, ALU.min, ALU.max).then_inc(clipped, 1)

            def rounding_constant(b):
                dve.wait_ge(clipped, b + 1)
                dve.tensor_scalar(cr[:].bitcast(U32), hn[:].bitcast(U32), EXPONENT, None,
                                  ALU.bitwise_and).then_inc(pow2, 1)
                dve.wait_ge(pow2, b + 1)
                dve.tensor_scalar(cr[:], cr[:], FP8_MIN_NORMAL, FP8_ROUND, ALU.max, ALU.mult).then_inc(round_c, 1)

            def finish_linear(b, half):
                dve.wait_ge(lin_done, 2 * b + half + 1)
                if half == 0:
                    dve.wait_ge(hb_ready, b + 1)
                    if past(b):
                        dve.wait_ge(stored, 16 * b)
                tok = slice(2 * half, 2 * half + 2)
                dve.scalar_tensor_tensor(out=y[:, tok, :].rearrange("p j d -> p (j d)"), in0=ps_m[:],
                                         scalar=s_in[:, 0:1], in1=hb[:, tok, :].rearrange("p j d -> p (j d)"),
                                         op0=ALU.mult, op1=ALU.add).then_inc(y_ready, 1)

            def slot(u, par, present):
                for s in range(STEPS):
                    if present(3):
                        if s == 4:
                            out_blocks(u - 3, 3)
                        if s in (9, 11):
                            add_residual(u - 3, s // 2 - 4)
                        if s in (29, 31):
                            finish_linear(u - 3, s // 2 - 14)
                    if present(2):
                        if s == 3:
                            split_max(u - 2, 1)
                        if s in (12, 20, 28):
                            out_blocks(u - 2, s // 8 - 1)
                    if s == 21 and present(1):
                        split_max(u - 1, 0)

                    if present(1):
                        maxima(u - 1, s)

                    if present(3):
                        if s == 4:
                            out_divide(u - 3, 3)
                        if s == 5:
                            out_back(u - 3, 1)
                        if s in (10, 12):
                            ln2_sum(u - 3, s - 10)
                            ln2_sum(u - 3, s - 9)
                        if s == 13:
                            ln2_finish(u - 3)
                        if s == 18:
                            clip(u - 3)
                        if s == 19:
                            rounding_constant(u - 3)
                    if present(0):
                        if s in (0, 1, 2, 3):
                            ln1_sum(u, par, s)
                        if s == 3:
                            ln1_finish(u)
                    if present(2):
                        if s in (13, 21, 29):
                            out_divide(u - 2, s // 8 - 1)
                        if s == 22:
                            out_back(u - 2, 0)

            run_slots(dve, slot)

        @block.gpsimd
        def _(pool):
            def settled():
                pool.sem_inc(met, 1)

            def layernorm_x(b, par):
                pool.wait_ge(ln1_ready, 2 * b + 2)
                pool.tensor_tensor(rs1[:], ve1[:], half_neg[:], ALU.pow).then_inc(rs1_ready, 1)
                pool.wait_ge(rs1_ready, b + 1)
                if past(b):
                    pool.wait_ge(xt_done, 2 * b)
                settled()
                for j in range(NJ):
                    last = pool.tensor_scalar(xn[:, j, :], xin[par][:, j, :], nm1[:, j:j + 1], rs1[:, j:j + 1],
                                              ALU.add, ALU.mult)
                last.then_inc(xn_ready, 1)

            def add_bias(b):
                pool.wait_ge(xr_in, 16 * b + 16)
                pool.tensor_tensor(xres[:], xres[:], b_proj[:].unsqueeze(1).to_broadcast([P, NJ, D]),
                                   ALU.add).then_inc(res_ready, 1)

            def split(b, par, n):
                pool.wait_ge(whole_ready, 4 * b + n + 1)
                if past(4 * b + n - 1):
                    pool.wait_ge(part3, 4 * b + n - 1)
                pool.tensor_tensor(rest[:, n % 2, :], whole[:, n % 2, :], parts[:, n, 0, :],
                                   ALU.subtract).then_inc(rest_ready, 1)
                pool.wait_ge(rest_ready, 4 * b + n + 1)
                if past(b):
                    pool.wait_ge(stacked[n // 2][1 - par], 96 * (b - 2 + par) + 192)
                settled()
                pool.tensor_scalar(parts[:, n, 1, :], rest[:, n % 2, :], 1.0, 0.0, ALU.mult,
                                   ALU.add).then_inc(part2, 1)
                pool.wait_ge(part2, 4 * b + n + 1)
                pool.tensor_tensor(parts[:, n, 2, :], rest[:, n % 2, :], parts[:, n, 1, :],
                                   ALU.subtract).then_inc(part3, 1)

            def layernorm_h(b):
                pool.wait_ge(ln2_ready, 2 * b + 2)
                pool.tensor_tensor(rs2[:], ve2[:], half_neg[:], ALU.pow).then_inc(rs2_pow, 1)
                pool.wait_ge(rs2_pow, b + 1)
                settled()
                pool.tensor_scalar(rs2[:], rs2[:], s_inv[:, 0:1], 0.0, ALU.mult, ALU.add).then_inc(rs2_ready, 1)
                pool.wait_ge(rs2_ready, b + 1)
                settled()
                for j in range(NJ):
                    last = pool.tensor_scalar(hn[:, j, :], h[:, j, :], nm2[:, j:j + 1], rs2[:, j:j + 1],
                                              ALU.add, ALU.mult)
                last.then_inc(hn_ready, 1)

            def add_linear_bias(b):
                pool.wait_ge(h_ready, 2 * b + 2)
                if past(b):
                    pool.wait_ge(y_ready, 2 * b)
                pool.tensor_tensor(hb[:], h[:], b_lin[:].unsqueeze(1).to_broadcast([P, NJ, D]),
                                   ALU.add).then_inc(hb_ready, 1)

            def round_fp8(b):
                pool.wait_ge(round_c, b + 1)
                pool.tensor_tensor(hn[:], hn[:], cr[:], ALU.add).then_inc(sum_c, 1)
                pool.wait_ge(sum_c, b + 1)
                if past(b):
                    pool.wait_ge(xq_done, b)
                pool.tensor_tensor(hq[:], hn[:], cr[:], ALU.subtract).then_inc(hq_ready, 1)

            def slot(u, par, present):
                if present(0):
                    layernorm_x(u, par)
                if present(3):
                    add_bias(u - 3)
                    layernorm_h(u - 3)
                    add_linear_bias(u - 3)
                if present(0):
                    split(u, par, 0)
                if present(3):
                    round_fp8(u - 3)
                if present(0):
                    for n in range(1, 4):
                        split(u, par, n)

            pool.wait_ge(half_set, 1)
            pool.wait_ge(const_v, 8)
            run_slots(pool, slot)


def kernel(L0_attn_x, L0_attn_qkv_w, L0_attn_qkv_b, L0_attn_proj_w, L0_attn_proj_b,
           L0_ffn_weight_fp8, L0_ffn_bias, L0_ffn_input_scale, L0_ffn_weight_scale):
    import numpy as np
    import concourse.bacc as bacc
    from concourse.bass_utils import run_bass_kernel_spmd

    order = np.arange(2 * D).reshape(2 * NT, HT, HD).transpose(0, 2, 1).reshape(-1)
    order = np.concatenate([order, np.arange(2 * D, 3 * D)])
    a = {k: np.asarray(v) for k, v in dict(
        x=L0_attn_x, qkv_wT=np.asarray(L0_attn_qkv_w)[order].T,
        qk_bT=np.asarray(L0_attn_qkv_b)[order[:2 * D]].reshape(2 * NT, P).T,
        v_bT=np.asarray(L0_attn_qkv_b)[2 * D:].reshape(NT, P).T,
        proj_wT=np.asarray(L0_attn_proj_w).T, proj_b=L0_attn_proj_b,
        lin_wT=np.asarray(L0_ffn_weight_fp8).T, lin_b=L0_ffn_bias,
        in_scale=L0_ffn_input_scale, w_scale=L0_ffn_weight_scale,
        eye=np.eye(P, dtype=np.float32)).items()}
    nc = bacc.Bacc("TRN2", target_bir_lowering=False, num_devices=1)
    arrays = {f"in_{k}": np.ascontiguousarray(v) for k, v in a.items()}
    args = [nc.dram_tensor(k, v.shape, mybir.dt.from_np(v.dtype), kind="ExternalInput").ap()
            for k, v in arrays.items()]
    out = nc.dram_tensor("out_0", (B, S, D), F32, kind="ExternalOutput").ap()
    block_kernel(nc, *args, out)
    r = run_bass_kernel_spmd(nc, [arrays], core_ids=[0])
    return r.results[0]["out_0"]
```

```python
from contextlib import ExitStack

import concourse.bass as bass
from concourse import mybir

F32 = mybir.dt.float32
BF16 = mybir.dt.bfloat16
F32R = mybir.dt.float32r
U32 = mybir.dt.uint32
ALU = mybir.AluOpType
ACT = mybir.ActivationFunctionType
AX_X = mybir.AxisListType.X

P = 128
B, S, D, H = 16, 512, 256, 16
HD = D // H
SCALE = float(HD) ** -0.5
EPS = 1e-5
NJ = S // P
NC = D // P
HT = P // HD
NT = H // HT
Q_PARTS = [0, 0, 1, 0, 2, 1]
K_PARTS = [0, 1, 0, 2, 0, 1]
PAIRS = [(0, 0), (0, 1), (1, 0)]
KR = HD * len(Q_PARTS)
KM = KR + 3
VW = 32
FP8_MAX = 448.0
FP8_MIN_NORMAL = 2.0 ** -6
FP8_ROUND = 1.5 * 2.0 ** 20
EXPONENT = 0x7F800000

STEPS = 32
UNITS = STEPS // 4
NSLOT = B + 3
LOOP_FROM, LOOP_TO = 4, 14


def block_kernel(nc, x, qkv_wT, qk_bT, v_bT, proj_wT, proj_b, lin_wT, lin_b, in_scale, w_scale, eye, out):
    x_d = x.rearrange("b (p j) d -> b p j d", j=NJ)
    out_d = out.rearrange("b (p j) d -> b p j d", j=NJ)

    with ExitStack() as ctx:
        def sb(name, shape, dt=F32):
            return ctx.enter_context(nc.sbuf_tensor(name, shape, dt))

        def ps(name, shape):
            return ctx.enter_context(nc.psum_tensor(name, shape, F32))

        def sem(name):
            return ctx.enter_context(nc.semaphore(name))

        wqkv_p = sb("wqkv_p", [P, 2, NC, 3 * D], F32R)
        wproj_p = sb("wproj_p", [P, 2, NC, D], F32R)
        wlin_p = sb("wlin_p", [P, 2, NC, D], F32R)
        b_qk = sb("b_qk", [P, 2 * NT])
        b_v = sb("b_v", [P, NT])
        b_proj = sb("b_proj", [P, D])
        b_lin = sb("b_lin", [P, D])
        s_in = sb("s_in", [P, 1])
        s_w = sb("s_w", [P, 1])
        s_inv = sb("s_inv", [P, 1])
        ident = sb("ident", [P, P])
        ident_b = sb("ident_b", [P, P], BF16)
        half_neg = sb("half_neg", [P, NJ])
        xin = [sb(f"xin{i}", [P, NJ, D]) for i in range(2)]
        st1 = sb("st1", [P, NJ, 6])
        mv1 = sb("mv1", [P, NJ, 2])
        nm1 = sb("nm1", [P, NJ])
        ve1 = sb("ve1", [P, NJ])
        rs1 = sb("rs1", [P, NJ])
        xn = sb("xn", [P, NJ, D])
        xnT = sb("xnT", [P, S])
        xnT_p = sb("xnT_p", [P, 2, NC, S], F32R)
        parts = sb("parts", [P, 2 * NT, 3, S], BF16)
        whole = sb("whole", [P, 2, S])
        qs = [sb(f"qs{i}", [P, H, S], BF16) for i in range(2)]
        ks = [sb(f"ks{i}", [P, H, S], BF16) for i in range(2)]
        vt = [sb(f"vt{i}", [P, NJ, H, VW]) for i in range(2)]
        mx = sb("mx", [P, NT, HT * NJ])
        nmax = sb("nmax", [HT * NJ, NT, 3, P], BF16)
        nmax_r = sb("nmax_r", [HT * NJ, P])
        pt = [sb(f"pt{i}", [P, 4, 2, S]) for i in range(2)]
        ot = sb("ot", [P, S // 32, 32])
        rden = sb("rden", [P, S // 32])
        on = sb("on", [P, S // 32, 32])
        oT = sb("oT", [P, S])
        oT_p = sb("oT_p", [P, 2, NT, S], F32R)
        xres = sb("xres", [P, NJ, D])
        h = sb("h", [P, NJ, D])
        st2 = sb("st2", [P, NJ, 6])
        mv2 = sb("mv2", [P, NJ, 2])
        nm2 = sb("nm2", [P, NJ])
        ve2 = sb("ve2", [P, NJ])
        rs2 = sb("rs2", [P, NJ])
        hn = sb("hn", [P, NJ, D])
        cr = xres
        hq = sb("hq", [P, NJ, D], BF16)
        hqT = sb("hqT", [P, NC, S], F32R)

        room = pt[0][:].rearrange("p i a n -> p (i a n)")
        wqkv = room[:, 0:NC * 3 * D].rearrange("p (c e) -> p c e", c=NC)
        wproj = room[:, NC * 3 * D:NC * 4 * D].rearrange("p (c e) -> p c e", c=NC)
        wlin = room[:, NC * 4 * D:NC * 5 * D].rearrange("p (c e) -> p c e", c=NC)
        wlin_rest = room[:, NC * 5 * D:NC * 6 * D].rearrange("p (c e) -> p c e", c=NC)

        b_v_rep = room[:, NC * 6 * D:NC * 6 * D + NT * P].rearrange("p (t m) -> p t m", t=NT)

        ps_t = ps("ps_t", [P, 2, S])
        ps_s = ps("ps_s", [P, 2, 2, S])
        ps_o = ps("ps_o", [P, S])
        ps_m = ps("ps_m", [P, S])

        w_in = sem("w_in")
        consts = sem("consts")
        wqkv_ready = sem("wqkv_ready")
        const_v = sem("const_v")
        bias_done = sem("bias_done")
        ones = sem("ones")
        ks_ones = sem("ks_ones")
        x_in = [sem(f"x_in{i}") for i in range(2)]
        xr_in = sem("xr_in")
        stacked = [[sem(f"stacked{t}{i}") for i in range(2)] for t in range(NT)]
        rows_in = [sem(f"rows_in{t}") for t in range(NT)]
        stored = sem("stored")
        met = sem("met")
        xt_done = sem("xt_done")
        qk_done = sem("qk_done")
        v_done = sem("v_done")
        s_done = sem("s_done")
        mt_done = sem("mt_done")
        st_done = sem("st_done")
        pv_done = sem("pv_done")
        proj_done = sem("proj_done")
        xq_done = sem("xq_done")
        lin_done = sem("lin_done")
        xnT_ready = sem("xnT_ready")
        xnT_high = sem("xnT_high")
        oT_high = sem("oT_high")
        part1 = sem("part1")
        whole_ready = sem("whole_ready")
        v_ready = sem("v_ready")
        exp_done = sem("exp_done")
        hqT_ready = sem("hqT_ready")
        ln1_sums = sem("ln1_sums")
        ln1_mv = sem("ln1_mv")
        ln1_ready = sem("ln1_ready")
        ln2_sums = sem("ln2_sums")
        ln2_mv = sem("ln2_mv")
        ln2_ready = sem("ln2_ready")
        max_done = sem("max_done")
        nmax_split = sem("nmax_split")
        ot_ready = sem("ot_ready")
        rden_ready = sem("rden_ready")
        on_ready = sem("on_ready")
        oT_ready = sem("oT_ready")
        h_ready = sem("h_ready")
        clipped = sem("clipped")
        pow2 = sem("pow2")
        round_c = sem("round_c")
        y_ready = sem("y_ready")
        half_set = sem("half_set")
        rs1_ready = sem("rs1_ready")
        xn_ready = sem("xn_ready")
        rest_ready = sem("rest_ready")
        part2 = sem("part2")
        xnT_low = sem("xnT_low")
        oT_low = sem("oT_low")
        part3 = sem("part3")
        res_ready = sem("res_ready")
        rs2_pow = sem("rs2_pow")
        rs2_ready = sem("rs2_ready")
        hn_ready = sem("hn_ready")
        hb_ready = sem("hb_ready")
        sum_c = sem("sum_c")
        hq_ready = sem("hq_ready")

        def past(count):
            return not isinstance(count, int) or count > 0

        def run_slots(eng, slot, prepare=None):
            def present(u):
                return lambda behind: 0 <= u - behind < B
            for u in range(LOOP_FROM):
                slot(u, u % 2, present(u))
                if u == 0 and prepare:
                    prepare()
            with eng.Fori(0, (LOOP_TO - LOOP_FROM) // 2) as i:
                for half in range(2):
                    slot(i * 2 + (LOOP_FROM + half), half, lambda behind: True)
            for u in range(LOOP_TO, NSLOT):
                slot(u, u % 2, present(u))

        block = ctx.enter_context(nc.Block())

        @block.sync
        def _(sp):
            sp.dma_start(xin[0][:], x_d[0]).then_inc(x_in[0], 16)
            for dst, src in ((ident[:], eye), (wqkv, qkv_wT.rearrange("(c p) e -> p c e", p=P)), (b_qk[:], qk_bT)):
                sp.dma_start(dst, src).then_inc(w_in, 16)
            for dst, src in ((wproj, proj_wT.rearrange("(c p) e -> p c e", p=P)), (b_v[:], v_bT),
                             (wlin, lin_wT.rearrange("(c p) e -> p c e", p=P)),
                             (b_proj[:], proj_b.partition_broadcast(P)),
                             (b_lin[:], lin_b.partition_broadcast(P)),
                             (s_in[:], in_scale.partition_broadcast(P)),
                             (s_w[:], w_scale.partition_broadcast(P))):
                sp.dma_start(dst, src).then_inc(consts, 16)

            def settled():
                sp.sem_inc(met, 1)

            def load(b, par):
                if past(b - 1):
                    sp.wait_ge(xn_ready, b - 1)
                settled()
                sp.dma_start(xin[par][:], x_d[bass.ds(b, 1)].rearrange("a p j d -> (a p) j d")).then_inc(x_in[par], 16)

            def reload(b, par):
                if past(b):
                    sp.wait_ge(hq_ready, b)
                settled()
                sp.dma_start(xres[:], x_d[bass.ds(b, 1)].rearrange("a p j d -> (a p) j d")).then_inc(xr_in, 16)

            def stack(b, par, t):
                sp.wait_ge(part3, 4 * b + 2 * t + 2)
                settled()
                if past(2 * STEPS * (b - 2) + (t + 1) * STEPS):
                    sp.wait_ge(st_done, 2 * STEPS * (b - 2) + (t + 1) * STEPS)
                settled()
                for r, (pq, pk) in enumerate(zip(Q_PARTS, K_PARTS)):
                    rows = slice(HD * r, HD * (r + 1))
                    for dst, src in ((qs, parts[:, 2 * t, pq, :]), (ks, parts[:, 2 * t + 1, pk, :])):
                        sp.dma_start(dst[par][rows, HT * t:HT * (t + 1), :], src).then_inc(stacked[t][par], 16)

            def rows(b, par, t):
                sp.wait_ge(nmax_split, 8 * b + 4 * t + 4)
                settled()
                for i in range(3):
                    sp.dma_start(qs[par][KR + i:KR + i + 1, HT * t:HT * (t + 1), :],
                                 nmax[:, t, i, :]).then_inc(rows_in[t], 16)

            def store(b, par):
                sp.wait_ge(y_ready, 2 * b + 2)
                settled()
                sp.dma_start(out_d[bass.ds(b, 1)].rearrange("a p j d -> (a p) j d"), h[:]).then_inc(stored, 16)

            def slot(u, par, present):
                if present(-1):
                    load(u + 1, 1 - par)
                if present(2):
                    rows(u - 2, par, 1)
                if present(0):
                    stack(u, par, 0)
                if present(1):
                    rows(u - 1, 1 - par, 0)
                if present(2):
                    reload(u - 2, par)
                if present(3):
                    store(u - 3, 1 - par)
                if present(0):
                    stack(u, par, 1)

            run_slots(sp, slot)
            sp.wait_ge(stored, 16 * B)

        @block.tensor
        def _(pe):
            bank_user = [None, 0, 0]

            def take_bank(u, name, n, behind):
                last, m, b = bank_user[0], bank_user[1], u - bank_user[2]
                if last in ("transpose_x", "project_qk", "project_v"):
                    reader, value = {"transpose_x": (xnT_ready, 2 * b), "project_qk": (whole_ready, 4 * b),
                                     "project_v": (v_ready, 2 * b)}[last]
                    pe.wait_ge(reader, value + m + 1)
                elif last == "transpose_max":
                    pe.wait_ge(nmax_split, 8 * b + 4 * m + 2)
                elif last == "project_out":
                    pe.wait_ge(h_ready, 2 * b + m + 1)
                elif last == "transpose_hq":
                    pe.wait_ge(hqT_ready, b + 1)
                elif last == "linear":
                    pe.wait_ge(y_ready, 2 * b + m + 1)
                elif last == "bias":
                    pe.wait_ge(const_v, 4)
                bank_user[:] = [name, n, behind]

            def transpose_x(u, c):
                take_bank(u, "transpose_x", c, 0)
                pe.wait_ge(xn_ready, u + 1)
                for j in range(NJ):
                    last = nc.tensor.transpose(ps_m[:, j * P:(j + 1) * P], xn[:, j, c * P:(c + 1) * P], ident[:])
                last.then_inc(xt_done, 1)

            def project_qk(u, n):
                take_bank(u, "project_qk", n, 0)
                if n == 0:
                    pe.wait_ge(xnT_low, 2 * u + 2)
                    if isinstance(u, int) and u == 0:
                        pe.wait_ge(wqkv_ready, 2)
                first = (n % 2) * D + (n // 2) * P
                for m, (pw, px) in enumerate(PAIRS):
                    for c in range(NC):
                        last = nc.tensor.matmul(ps_m[:], wqkv_p[:, pw, c, first:first + P], xnT_p[:, px, c, :],
                                                start=(m == 0 and c == 0), stop=(m == 2 and c == NC - 1))
                last.then_inc(qk_done, 1)

            def project_v(u, half):
                take_bank(u, "project_v", half, 1)
                for j in range(2):
                    tok = slice((2 * half + j) * P, (2 * half + j + 1) * P)
                    for m, (pw, px) in enumerate(PAIRS):
                        for c in range(NC):
                            last = nc.tensor.matmul(ps_m[:, j * D:(j + 1) * D], xnT_p[:, px, c, tok],
                                                    wqkv_p[:, pw, c, 2 * D:3 * D],
                                                    start=(m == 0 and c == 0), stop=(m == 2 and c == NC - 1))
                last.then_inc(v_done, 1)

            def transpose_max(u, t, behind):
                take_bank(u, "transpose_max", t, behind)
                pe.wait_ge(max_done, STEPS * (u - behind) + (t + 1) * STEPS // 2)
                nc.tensor.transpose(ps_m[0:HT * NJ, 0:P], mx[:, t, :], ident[:]).then_inc(mt_done, 1)

            def project_out(u, half):
                take_bank(u, "project_out", half, 3)
                if isinstance(u, int) and u == 3:
                    pe.wait_ge(const_v, 9)
                if half == 0:
                    pe.wait_ge(oT_low, NT * (u - 3) + NT)
                for j in range(2):
                    tok = slice((2 * half + j) * P, (2 * half + j + 1) * P)
                    for m, (pw, px) in enumerate(PAIRS):
                        for t in range(NT):
                            last = nc.tensor.matmul(ps_m[:, j * D:(j + 1) * D], oT_p[:, px, t, tok],
                                                    wproj_p[:, pw, t, :],
                                                    start=(m == 0 and t == 0), stop=(m == 2 and t == NT - 1))
                last.then_inc(proj_done, 1)

            def transpose_hq(u):
                take_bank(u, "transpose_hq", 0, 3)
                if isinstance(u, int) and u == 3:
                    pe.wait_ge(const_v, 9)
                pe.wait_ge(hq_ready, u - 3 + 1)
                psb = ps_m[:].bitcast(BF16)
                for c in range(NC):
                    for j in range(NJ):
                        last = nc.tensor.transpose(psb[:, c * S + j * P:c * S + (j + 1) * P],
                                                   hq[:, j, c * P:(c + 1) * P], ident_b[:])
                last.then_inc(xq_done, 1)

            def linear(u, half):
                if isinstance(u, int) and u == 3:
                    pe.wait_ge(const_v, 9)
                take_bank(u, "linear", half, 3)
                if half == 0:
                    pe.wait_ge(hqT_ready, u - 3 + 1)
                for j in range(2):
                    tok = slice((2 * half + j) * P, (2 * half + j + 1) * P)
                    for c in range(NC):
                        for part in range(2):
                            last = nc.tensor.matmul(ps_m[:, j * D:(j + 1) * D], hqT[:, c, tok], wlin_p[:, part, c, :],
                                                    start=(c == 0 and part == 0),
                                                    stop=(c == NC - 1 and part == 1))
                last.then_inc(lin_done, 1)

            def scores_t(b, par, s, a):
                n, i = s // 4, s % 4
                t, odd, kp = n // 4, n // 2 % 2, n % 2
                head = HT * t + 2 * i + odd
                if s in (0, STEPS // 2) and a == 0:
                    pe.wait_ge(rows_in[t], 48 * b + 48)
                    if isinstance(b, int) and b == 0:
                        pe.wait_ge(ks_ones, 2)
                if past(2 * STEPS * b + 2 * s + a - 1):
                    pe.wait_ge(exp_done, 2 * STEPS * b + 2 * s + a - 1)
                keys = slice((2 * kp + a) * P, (2 * kp + a + 1) * P)
                nc.tensor.matmul(ps_t[:, a, :], ks[par][0:KM, head, keys], qs[par][0:KM, head, :],
                                 start=True, stop=True).then_inc(st_done, 1)

            def scores(b, par, s, a):
                head = s // 2
                if s in (0, STEPS // 2) and a == 0:
                    t = s // (STEPS // 2)
                    pe.wait_ge(stacked[t][par], 96 * (b - par) + 192)
                if a == 0 and past(STEPS * b + s - 1):
                    pe.wait_ge(max_done, STEPS * b + s - 1)
                queries = slice((2 * (s % 2) + a) * P, (2 * (s % 2) + a + 1) * P)
                last = nc.tensor.matmul(ps_s[:, s % 2, a, :], qs[par][0:KR, head, queries],
                                        ks[par][0:KR, head, :], start=True, stop=True)
                if a == 1:
                    last.then_inc(s_done, 1)

            def values(b, par, n, a):
                t, odd, kp = n // 4, n // 2 % 2, n % 2
                if a == 0:
                    if n == 0:
                        pe.wait_ge(v_ready, 2 * b + 2)
                    pe.wait_ge(exp_done, 2 * (STEPS * b + 4 * n + 4))
                    if kp == 0:
                        if past(4 * b + n // 2):
                            pe.wait_ge(ot_ready, 4 * b + n // 2)
                for i in range(4):
                    head = HT * t + 2 * i + odd
                    last = nc.tensor.matmul(ps_o[32 * i:32 * i + VW, :], vt[par][:, 2 * kp + a, head, :],
                                            pt[n % 2][:, i, a, :], start=(kp == 0 and a == 0),
                                            stop=(kp == 1 and a == 1))
                if a == 1:
                    last.then_inc(pv_done, 1)

            def slot(u, par, present):
                bank_user[2] += 1
                for s in range(STEPS):
                    if present(2):
                        scores_t(u - 2, par, s, 0)
                    if present(1):
                        scores(u - 1, 1 - par, s, 0)
                    if s == 2 and present(2):
                        transpose_max(u, 1, 2)
                    if s in (4, 6) and present(1):
                        project_v(u, s // 2 - 2)
                    if s in (8, 10) and present(3):
                        project_out(u, s // 2 - 4)
                    if s in (12, 14) and present(0):
                        transpose_x(u, s // 2 - 6)
                    if s in (16, 18) and present(0):
                        project_qk(u, s // 2 - 8)
                    if s == 20 and present(1):
                        transpose_max(u, 0, 1)
                    if s in (22, 24) and present(0):
                        project_qk(u, s // 2 - 9)
                    if s == 26 and present(3):
                        transpose_hq(u)
                    if s in (28, 30) and present(3):
                        linear(u, s // 2 - 14)
                    if s % 2:
                        n = s // 4 - 1
                        if n >= 0 and present(2):
                            values(u - 2, par, n, s // 2 % 2)
                        if n < 0 and present(3):
                            values(u - 3, 1 - par, UNITS - 1, s // 2 % 2)
                    if present(2):
                        scores_t(u - 2, par, s, 1)
                    if present(1):
                        scores(u - 1, 1 - par, s, 1)

            def prepare():
                pe.wait_ge(consts, 16 * 7)
                pe.wait_ge(const_v, 2)
                take_bank(0, "bias", 0, 0)
                for t in range(NT):
                    last = nc.tensor.matmul(ps_m[:, 0:D], b_v_rep[:, t, :], wproj[:, t, :],
                                            start=(t == 0), stop=(t == NT - 1))
                last.then_inc(bias_done, 1)

            pe.wait_ge(w_in, 48)
            run_slots(pe, slot, prepare)

        @block.scalar
        def _(act):
            def exps(b, s, a):
                n, i = s // 4, s % 4
                if i == 0 and a == 0 and past(UNITS * b + n - 1):
                    act.wait_ge(pv_done, UNITS * b + n - 1)
                if isinstance(b, int) and b == 0 and s == 0:
                    act.wait_ge(const_v, 9)
                act.wait_ge(st_done, 2 * (STEPS * b + s) + a + 1)
                nc.scalar.activation(pt[n % 2][:, i, a, :], ps_t[:, a, :], ACT.Exp, scale=SCALE).then_inc(exp_done, 1)

            def copy_v(b, par, half):
                act.wait_ge(v_done, 2 * b + half + 1)
                if isinstance(b, int) and b == 0:
                    act.wait_ge(ones, 2)
                if past(UNITS * (b - 1)):
                    act.wait_ge(pv_done, UNITS * (b - 1))
                nc.scalar.copy(vt[par][:, 2 * half:2 * half + 2, :, 0:HD],
                               ps_m[:].rearrange("p (j h e) -> p j h e", j=2, h=H)).then_inc(v_ready, 1)

            def copy_xnT(b, c):
                act.wait_ge(xt_done, 2 * b + c + 1)
                if past(b):
                    act.wait_ge(v_done, 2 * b)
                nc.scalar.copy(xnT_p[:, 0, c, :], ps_m[:]).then_inc(xnT_high, 1)
                if past(2 * b + c):
                    act.wait_ge(xnT_low, 2 * b + c)
                nc.scalar.copy(xnT[:], ps_m[:]).then_inc(xnT_ready, 1)

            def copy_oT(b, t):
                act.wait_ge(oT_ready, NT * b + t + 1)
                if past(b):
                    act.wait_ge(proj_done, 2 * b)
                nc.scalar.copy(oT_p[:, 0, t, :], oT[:]).then_inc(oT_high, 1)

            def copy_qk(b, par, n):
                t, bias = n // 2, b_qk[:, (n % 2) * NT + n // 2:(n % 2) * NT + n // 2 + 1]
                act.wait_ge(qk_done, 4 * b + n + 1)
                if past(b):
                    act.wait_ge(stacked[t][1 - par], 96 * (b - 2 + par) + 192)
                nc.scalar.activation(parts[:, n, 0, :], ps_m[:], ACT.Identity, bias=bias).then_inc(part1, 1)
                if past(4 * b + n - 1):
                    act.wait_ge(part3, 4 * b + n - 1)
                nc.scalar.activation(whole[:, n % 2, :], ps_m[:], ACT.Identity, bias=bias).then_inc(whole_ready, 1)

            def copy_hqT(b):
                act.wait_ge(xq_done, b + 1)
                if past(b):
                    act.wait_ge(lin_done, 2 * b)
                nc.scalar.copy(hqT[:].rearrange("p c n -> p (c n)"), ps_m[:].bitcast(BF16)).then_inc(hqT_ready, 1)

            def slot(u, par, present):
                for s in range(STEPS):
                    if present(2):
                        exps(u - 2, s, 0)
                    if s == 6 and present(3):
                        copy_oT(u - 3, 1)
                    if s == 23 and present(2):
                        copy_oT(u - 2, 0)
                    if s in (4, 6) and present(1):
                        copy_v(u - 1, 1 - par, s // 2 - 2)
                    if s in (12, 14) and present(0):
                        copy_xnT(u, s // 2 - 6)
                    if s in (16, 18) and present(0):
                        copy_qk(u, par, s // 2 - 8)
                    if s in (22, 24) and present(0):
                        copy_qk(u, par, s // 2 - 9)
                    if s == 26 and present(3):
                        copy_hqT(u - 3)
                    if present(2):
                        exps(u - 2, s, 1)

            act.wait_ge(w_in, 48)
            run_slots(act, slot)

        @block.vector
        def _(dve):
            def prepare():
                dve.memset(half_neg[:], -0.5).then_inc(half_set, 1)
                dve.wait_ge(w_in, 48)
                dve.tensor_copy(wqkv_p[:, 0], wqkv).then_inc(wqkv_ready, 1)
                dve.wait_ge(wqkv_ready, 1)
                dve.tensor_tensor(wqkv_p[:, 1], wqkv, wqkv_p[:, 0].bitcast(F32), ALU.subtract).then_inc(wqkv_ready, 1)

            def prepare_more():
                dve.wait_ge(consts, 16 * 7)
                dve.reciprocal(s_inv[:], s_in[:]).then_inc(const_v, 1)
                dve.tensor_copy(b_v_rep, b_v[:].unsqueeze(2).to_broadcast([P, NT, P])).then_inc(const_v, 1)
                dve.memset(vt[0][:], 1.0).then_inc(ones, 1)
                dve.memset(vt[1][:], 1.0).then_inc(ones, 1)
                dve.tensor_copy(wproj_p[:, 0], wproj).then_inc(const_v, 1)
                dve.wait_ge(bias_done, 1)
                dve.tensor_tensor(b_proj[:], ps_m[:, 0:D], b_proj[:], ALU.add).then_inc(const_v, 1)
                dve.wait_ge(const_v, 3)
                dve.tensor_tensor(wproj_p[:, 1], wproj, wproj_p[:, 0].bitcast(F32), ALU.subtract).then_inc(const_v, 1)
                dve.tensor_copy(ident_b[:], ident[:]).then_inc(const_v, 1)
                dve.tensor_scalar(wlin_rest, wlin, s_w[:, 0:1], None, ALU.mult).then_inc(const_v, 1)
                dve.wait_ge(const_v, 7)
                dve.tensor_copy(wlin_p[:, 0], wlin_rest).then_inc(const_v, 1)
                dve.wait_ge(const_v, 8)
                dve.tensor_tensor(wlin_p[:, 1], wlin_rest, wlin_p[:, 0].bitcast(F32), ALU.subtract).then_inc(const_v, 1)

            def maxima(b, s):
                t = s // (STEPS // 2)
                if s in (0, STEPS // 2) and past(NT * (b - 1) + t + 1):
                    dve.wait_ge(mt_done, NT * (b - 1) + t + 1)
                dve.wait_ge(s_done, STEPS * b + s + 1)
                col = 2 * (s % (STEPS // 2))
                dve.tensor_reduce(mx[:, t, col:col + 2], ps_s[:, s % 2, :, :], AX_X, ALU.max).then_inc(max_done, 1)

            def ln1_sum(b, par, j):
                if j == 0:
                    dve.wait_ge(x_in[par], 8 * (b - par) + 16)
                    if past(b):
                        dve.wait_ge(xn_ready, b)
                dve.bn_stats(st1[:, j, :], xin[par][:, j, :]).then_inc(ln1_sums, 1)

            def ln1_finish(b):
                dve.wait_ge(ln1_sums, NJ * b + NJ)
                dve.sem_inc(met, 1)
                for j in range(NJ):
                    last = dve.bn_aggr(mv1[:, j, :], st1[:, j, :])
                last.then_inc(ln1_mv, 1)
                dve.wait_ge(ln1_mv, b + 1)
                dve.tensor_scalar(nm1[:], mv1[:, :, 0], -1.0, None, ALU.mult).then_inc(ln1_ready, 1)
                dve.tensor_scalar(ve1[:], mv1[:, :, 1], EPS, None, ALU.add).then_inc(ln1_ready, 1)

            def ln2_sum(b, j):
                if j == 0 and past(b):
                    dve.wait_ge(hn_ready, b)
                if j % 2 == 0:
                    dve.wait_ge(h_ready, 2 * b + j // 2 + 1)
                    dve.sem_inc(met, 1)
                dve.bn_stats(st2[:, j, :], h[:, j, :]).then_inc(ln2_sums, 1)

            def ln2_finish(b):
                dve.wait_ge(ln2_sums, NJ * b + NJ)
                dve.sem_inc(met, 1)
                for j in range(NJ):
                    last = dve.bn_aggr(mv2[:, j, :], st2[:, j, :])
                last.then_inc(ln2_mv, 1)
                dve.wait_ge(ln2_mv, b + 1)
                dve.tensor_scalar(nm2[:], mv2[:, :, 0], -1.0, None, ALU.mult).then_inc(ln2_ready, 1)
                dve.tensor_scalar(ve2[:], mv2[:, :, 1], EPS, None, ALU.add).then_inc(ln2_ready, 1)

            def split_max(b, t):
                dve.wait_ge(mt_done, NT * b + t + 1)
                if past(b):
                    dve.wait_ge(rows_in[t], 48 * b)
                mT = ps_m[0:HT * NJ, 0:P]
                dve.tensor_scalar(nmax[:, t, 0, :], mT, -1.0, None, ALU.mult).then_inc(nmax_split, 1)
                dve.wait_ge(nmax_split, 8 * b + 4 * t + 1)
                dve.scalar_tensor_tensor(out=nmax_r[:], in0=mT, scalar=-1.0, in1=nmax[:, t, 0, :],
                                         op0=ALU.mult, op1=ALU.subtract).then_inc(nmax_split, 1)
                dve.wait_ge(nmax_split, 8 * b + 4 * t + 2)
                dve.tensor_copy(nmax[:, t, 1, :], nmax_r[:]).then_inc(nmax_split, 1)
                dve.wait_ge(nmax_split, 8 * b + 4 * t + 3)
                dve.tensor_tensor(nmax[:, t, 2, :], nmax_r[:], nmax[:, t, 1, :], ALU.subtract).then_inc(nmax_split, 1)

            def out_blocks(b, g):
                dve.wait_ge(pv_done, UNITS * b + 2 * g + 2)
                if past(4 * b + g):
                    dve.wait_ge(on_ready, 4 * b + g)
                dve.transpose(ot[:].rearrange("p a c -> p (a c)"), ps_o[:]).then_inc(ot_ready, 1)

            def out_reciprocal(b, g):
                dve.wait_ge(ot_ready, 4 * b + g + 1)
                dve.reciprocal(rden[:], ot[:, :, HD]).then_inc(rden_ready, 1)

            def out_back(b, t):
                dve.wait_ge(on_ready, 4 * b + 2 * t + 2)
                if past(NT * b + t):
                    dve.wait_ge(oT_low, NT * b + t)
                dve.transpose(oT[:], on[:].rearrange("p a c -> p (a c)")).then_inc(oT_ready, 1)

            def add_residual(b, half):
                dve.wait_ge(proj_done, 2 * b + half + 1)
                if half == 0:
                    dve.wait_ge(res_ready, b + 1)
                    if past(b):
                        dve.wait_ge(stored, 16 * b)
                tok = slice(2 * half, 2 * half + 2)
                dve.tensor_tensor(h[:, tok, :].rearrange("p j d -> p (j d)"), ps_m[:],
                                  xres[:, tok, :].rearrange("p j d -> p (j d)"), ALU.add).then_inc(h_ready, 1)

            def power_of_two(b):
                dve.wait_ge(clipped, b + 1)
                dve.tensor_scalar(cr[:].bitcast(U32), hn[:].bitcast(U32), EXPONENT, None,
                                  ALU.bitwise_and).then_inc(pow2, 1)

            def rounding_constant(b):
                dve.wait_ge(pow2, b + 1)
                dve.tensor_scalar(cr[:], cr[:], FP8_MIN_NORMAL, FP8_ROUND, ALU.max, ALU.mult).then_inc(round_c, 1)

            def finish_linear(b, half):
                dve.wait_ge(lin_done, 2 * b + half + 1)
                if half == 0:
                    dve.wait_ge(hb_ready, b + 1)
                tok = slice(2 * half, 2 * half + 2)
                dve.scalar_tensor_tensor(out=h[:, tok, :].rearrange("p j d -> p (j d)"), in0=ps_m[:],
                                         scalar=s_in[:, 0:1], in1=h[:, tok, :].rearrange("p j d -> p (j d)"),
                                         op0=ALU.mult, op1=ALU.add).then_inc(y_ready, 1)

            def slot(u, par, present):
                for s in range(STEPS):
                    if present(3):
                        if s == 3:
                            out_blocks(u - 3, 3)
                        if s in (8, 10):
                            add_residual(u - 3, s // 2 - 4)
                        if s in (28, 30):
                            finish_linear(u - 3, s // 2 - 14)
                    if present(2):
                        if s == 2:
                            split_max(u - 2, 1)
                        if s in (11, 19, 27):
                            out_blocks(u - 2, s // 8 - 1)
                    if s == 20 and present(1):
                        split_max(u - 1, 0)

                    if present(1):
                        maxima(u - 1, s)

                    if present(3):
                        if s == 3:
                            out_reciprocal(u - 3, 3)
                        if s == 5:
                            out_back(u - 3, 1)
                        if s in (9, 12):
                            ln2_sum(u - 3, 2 * (s // 12))
                            ln2_sum(u - 3, 2 * (s // 12) + 1)
                        if s == 13:
                            ln2_finish(u - 3)
                        if s == 17:
                            power_of_two(u - 3)
                        if s == 18:
                            rounding_constant(u - 3)
                    if present(0):
                        if s in (0, 1, 4, 6):
                            ln1_sum(u, par, (0, 1, 4, 6).index(s))
                        if s == 7:
                            ln1_finish(u)
                    if present(2):
                        if s in (11, 19, 27):
                            out_reciprocal(u - 2, s // 8 - 1)
                        if s == 22:
                            out_back(u - 2, 0)

            prepare()
            run_slots(dve, slot, prepare_more)

        @block.gpsimd
        def _(pool):
            def settled():
                pool.sem_inc(met, 1)

            def layernorm_x(b, par):
                pool.wait_ge(ln1_ready, 2 * b + 2)
                pool.tensor_tensor(rs1[:], ve1[:], half_neg[:], ALU.pow).then_inc(rs1_ready, 1)
                pool.wait_ge(rs1_ready, b + 1)
                if past(b):
                    pool.wait_ge(xt_done, 2 * b)
                settled()
                for j in range(NJ):
                    last = pool.tensor_scalar(xn[:, j, :], xin[par][:, j, :], nm1[:, j:j + 1], rs1[:, j:j + 1],
                                              ALU.add, ALU.mult)
                last.then_inc(xn_ready, 1)

            def low_xnT(b, c):
                pool.wait_ge(xnT_ready, 2 * b + c + 1)
                if past(b):
                    pool.wait_ge(v_done, 2 * b)
                pool.tensor_tensor(xnT_p[:, 1, c, :], xnT[:], xnT_p[:, 0, c, :].bitcast(F32),
                                   ALU.subtract).then_inc(xnT_low, 1)

            def low_oT(b, t):
                pool.wait_ge(oT_high, NT * b + t + 1)
                if past(b):
                    pool.wait_ge(proj_done, 2 * b)
                pool.tensor_tensor(oT_p[:, 1, t, :], oT[:], oT_p[:, 0, t, :].bitcast(F32),
                                   ALU.subtract).then_inc(oT_low, 1)

            def add_bias(b):
                pool.wait_ge(xr_in, 16 * b + 16)
                if isinstance(b, int) and b == 0:
                    pool.wait_ge(const_v, 9)
                pool.tensor_tensor(xres[:], xres[:], b_proj[:].unsqueeze(1).to_broadcast([P, NJ, D]),
                                   ALU.add).then_inc(res_ready, 1)

            def split(b, par, n):
                pool.wait_ge(whole_ready, 4 * b + n + 1)
                pool.tensor_tensor(whole[:, n % 2, :], whole[:, n % 2, :], parts[:, n, 0, :],
                                   ALU.subtract).then_inc(rest_ready, 1)
                pool.wait_ge(rest_ready, 4 * b + n + 1)
                if past(b):
                    pool.wait_ge(stacked[n // 2][1 - par], 96 * (b - 2 + par) + 192)
                settled()
                pool.tensor_scalar(parts[:, n, 1, :], whole[:, n % 2, :], 1.0, 0.0, ALU.mult,
                                   ALU.add).then_inc(part2, 1)
                pool.wait_ge(part2, 4 * b + n + 1)
                pool.tensor_tensor(parts[:, n, 2, :], whole[:, n % 2, :], parts[:, n, 1, :],
                                   ALU.subtract).then_inc(part3, 1)

            def out_divide(b, g):
                pool.wait_ge(rden_ready, 4 * b + g + 1)
                if g % 2 == 0 and past(NT * b + g // 2):
                    pool.wait_ge(oT_ready, NT * b + g // 2)
                half = slice(HD * (g % 2), HD * (g % 2) + HD)
                pool.tensor_tensor(on[:, :, half], ot[:, :, 0:HD], rden[:].unsqueeze(2).to_broadcast([P, S // 32, HD]),
                                   ALU.mult).then_inc(on_ready, 1)

            def layernorm_h(b):
                pool.wait_ge(ln2_ready, 2 * b + 2)
                pool.tensor_tensor(rs2[:], ve2[:], half_neg[:], ALU.pow).then_inc(rs2_pow, 1)
                pool.wait_ge(rs2_pow, b + 1)
                settled()
                pool.tensor_scalar(rs2[:], rs2[:], s_inv[:, 0:1], 0.0, ALU.mult, ALU.add).then_inc(rs2_ready, 1)
                pool.wait_ge(rs2_ready, b + 1)
                settled()
                for j in range(NJ):
                    last = pool.tensor_scalar(hn[:, j, :], h[:, j, :], nm2[:, j:j + 1], rs2[:, j:j + 1],
                                              ALU.add, ALU.mult)
                last.then_inc(hn_ready, 1)
                pool.wait_ge(hn_ready, b + 1)
                settled()
                pool.tensor_scalar(hn[:], hn[:], FP8_MAX, -FP8_MAX, ALU.min, ALU.max).then_inc(clipped, 1)

            def add_linear_bias(b):
                pool.wait_ge(hn_ready, b + 1)
                pool.tensor_tensor(h[:], h[:], b_lin[:].unsqueeze(1).to_broadcast([P, NJ, D]),
                                   ALU.add).then_inc(hb_ready, 1)

            def round_fp8(b):
                pool.wait_ge(round_c, b + 1)
                pool.tensor_tensor(hn[:], hn[:], cr[:], ALU.add).then_inc(sum_c, 1)
                pool.wait_ge(sum_c, b + 1)
                if past(b):
                    pool.wait_ge(xq_done, b)
                pool.tensor_tensor(hq[:], hn[:], cr[:], ALU.subtract).then_inc(hq_ready, 1)

            def slot(u, par, present):
                if present(3):
                    out_divide(u - 3, 3)
                    low_oT(u - 3, 1)
                    add_bias(u - 3)
                if present(0):
                    layernorm_x(u, par)
                    low_xnT(u, 0)
                if present(2):
                    out_divide(u - 2, 0)
                if present(0):
                    low_xnT(u, 1)
                if present(3):
                    layernorm_h(u - 3)
                if present(0):
                    split(u, par, 0)
                if present(3):
                    round_fp8(u - 3)
                if present(2):
                    out_divide(u - 2, 1)
                if present(0):
                    split(u, par, 1)
                if present(2):
                    low_oT(u - 2, 0)
                if present(3):
                    add_linear_bias(u - 3)
                if present(0):
                    split(u, par, 2)
                    split(u, par, 3)
                if present(2):
                    out_divide(u - 2, 2)

            def prepare():
                pool.wait_ge(part3, 4)
                pool.memset(ks[0][KR:KM, :, :], 1.0).then_inc(ks_ones, 1)
                pool.wait_ge(ks_ones, 1)
                pool.memset(ks[1][KR:KM, :, :], 1.0).then_inc(ks_ones, 1)
                pool.wait_ge(ks_ones, 2)

            pool.wait_ge(half_set, 1)
            run_slots(pool, slot, prepare)


def kernel(L0_attn_x, L0_attn_qkv_w, L0_attn_qkv_b, L0_attn_proj_w, L0_attn_proj_b,
           L0_ffn_weight_fp8, L0_ffn_bias, L0_ffn_input_scale, L0_ffn_weight_scale):
    import numpy as np
    import concourse.bacc as bacc
    from concourse.bass_utils import run_bass_kernel_spmd

    order = np.arange(2 * D).reshape(2 * NT, HT, HD).transpose(0, 2, 1).reshape(-1)
    order = np.concatenate([order, np.arange(2 * D, 3 * D)])
    a = {k: np.asarray(v) for k, v in dict(
        x=L0_attn_x, qkv_wT=np.asarray(L0_attn_qkv_w)[order].T,
        qk_bT=np.asarray(L0_attn_qkv_b)[order[:2 * D]].reshape(2 * NT, P).T,
        v_bT=np.asarray(L0_attn_qkv_b)[2 * D:].reshape(NT, P).T,
        proj_wT=np.asarray(L0_attn_proj_w).T, proj_b=L0_attn_proj_b,
        lin_wT=np.asarray(L0_ffn_weight_fp8).T, lin_b=L0_ffn_bias,
        in_scale=L0_ffn_input_scale, w_scale=L0_ffn_weight_scale,
        eye=np.eye(P, dtype=np.float32)).items()}
    nc = bacc.Bacc("TRN2", target_bir_lowering=False, num_devices=1)
    arrays = {f"in_{k}": np.ascontiguousarray(v) for k, v in a.items()}
    args = [nc.dram_tensor(k, v.shape, mybir.dt.from_np(v.dtype), kind="ExternalInput").ap()
            for k, v in arrays.items()]
    out = nc.dram_tensor("out_0", (B, S, D), F32, kind="ExternalOutput").ap()
    block_kernel(nc, *args, out)
    r = run_bass_kernel_spmd(nc, [arrays], core_ids=[0])
    return r.results[0]["out_0"]
```

```python
from contextlib import ExitStack

import concourse.bass as bass
from concourse import mybir

F32 = mybir.dt.float32
BF16 = mybir.dt.bfloat16
F32R = mybir.dt.float32r
U32 = mybir.dt.uint32
ALU = mybir.AluOpType
ACT = mybir.ActivationFunctionType
AX_X = mybir.AxisListType.X

P = 128
B, S, D, H = 16, 512, 256, 16
HD = D // H
SCALE = float(HD) ** -0.5
EPS = 1e-5
NJ = S // P
NC = D // P
HT = P // HD
NT = H // HT
Q_PARTS = [0, 0, 1, 0, 2, 1]
K_PARTS = [0, 1, 0, 2, 0, 1]
PAIRS = [(0, 0), (0, 1), (1, 0)]
KR = HD * len(Q_PARTS)
KM = KR + 3
VW = 32
FP8_MAX = 448.0
FP8_MIN_NORMAL = 2.0 ** -6
FP8_ROUND = 1.5 * 2.0 ** 20
EXPONENT = 0x7F800000

STEPS = 32
UNITS = STEPS // 4
NSLOT = B + 3
LOOP_FROM, LOOP_TO = 4, 14

PROJECT_V = (4, 6)
PROJECT_OUT = (8, 10)
TRANSPOSE_X = (12, 14)
PROJECT_QK = (16, 18, 20, 22)
TRANSPOSE_MAX = (25, 5)
TRANSPOSE_HQ = 26
LINEAR = (28, 30)
OUT_BLOCKS = (11, 19, 27, 3)
OUT_BACK = (22, 5)
COPY_OT = (24, 6)
LN1_SUM = (5, 7, 15, 17)
LN1_END = 29
LN2_SUM = (9, 9, 12, 12)
LN2_END = 13
POWER_OF_TWO = 18
ROUNDING_CONSTANT = 20


def block_kernel(nc, x, qkv_wT, qk_bT, v_bT, proj_wT, proj_b, lin_wT, lin_b, in_scale, w_scale, eye, out):
    x_d = x.rearrange("b (p j) d -> b p j d", j=NJ)
    out_d = out.rearrange("b (p j) d -> b p j d", j=NJ)

    with ExitStack() as ctx:
        def sb(name, shape, dt=F32):
            return ctx.enter_context(nc.sbuf_tensor(name, shape, dt))

        def ps(name, shape):
            return ctx.enter_context(nc.psum_tensor(name, shape, F32))

        def sem(name):
            return ctx.enter_context(nc.semaphore(name))

        wqkv_p = sb("wqkv_p", [P, 2, NC, 3 * D], F32R)
        wproj_p = sb("wproj_p", [P, 2, NC, D], F32R)
        wlin_p = sb("wlin_p", [P, 2, NC, D], F32R)
        b_qk = sb("b_qk", [P, 2 * NT])
        b_v = sb("b_v", [P, NT])
        b_proj = sb("b_proj", [P, D])
        b_lin = sb("b_lin", [P, D])
        s_in = sb("s_in", [P, 1])
        s_w = sb("s_w", [P, 1])
        s_inv = sb("s_inv", [P, 1])
        ident = sb("ident", [P, P])
        ident_b = sb("ident_b", [P, P], BF16)
        half_neg = sb("half_neg", [P, NJ])
        table = sb("table", [P, 1])
        xin = [sb(f"xin{i}", [P, NJ, D]) for i in range(2)]
        st1 = sb("st1", [P, NJ, 6])
        mv1 = sb("mv1", [P, NJ, 2])
        nm1 = sb("nm1", [P, NJ])
        ve1 = sb("ve1", [P, NJ])
        rs1 = sb("rs1", [P, NJ])
        xn = sb("xn", [P, NJ, D])
        xnT = sb("xnT", [P, S])
        xnT_p = sb("xnT_p", [P, 2, NC, S], F32R)
        parts = sb("parts", [P, 2 * NT, 3, S], BF16)
        whole = sb("whole", [P, 2, S])
        qs = [sb(f"qs{i}", [P, H, S], BF16) for i in range(2)]
        ks = [sb(f"ks{i}", [P, H, S], BF16) for i in range(2)]
        vt = [sb(f"vt{i}", [P, NJ, H, VW]) for i in range(2)]
        mx = sb("mx", [P, NT, HT * NJ])
        nmax = sb("nmax", [HT * NJ, NT, 3, P], BF16)
        nmax_r = sb("nmax_r", [HT * NJ, P])
        pt = [sb(f"pt{i}", [P, 4, 2, S]) for i in range(2)]
        ot = sb("ot", [P, S // 32, 32])
        rden = sb("rden", [P, S // 32])
        on = sb("on", [P, S // 32, 32])
        oT = sb("oT", [P, S])
        oT_p = sb("oT_p", [P, 2, NT, S], F32R)
        xres = sb("xres", [P, NJ, D])
        h = sb("h", [P, NJ, D])
        st2 = sb("st2", [P, NJ, 6])
        mv2 = sb("mv2", [P, NJ, 2])
        nm2 = sb("nm2", [P, NJ])
        ve2 = sb("ve2", [P, NJ])
        rs2 = sb("rs2", [P, NJ])
        hn = sb("hn", [P, NJ, D])
        cr = xres
        hq = sb("hq", [P, NJ, D], BF16)
        hqT = sb("hqT", [P, NC, S], F32R)

        room = pt[0][:].rearrange("p i a n -> p (i a n)")
        wqkv = room[:, 0:NC * 3 * D].rearrange("p (c e) -> p c e", c=NC)
        wproj = room[:, NC * 3 * D:NC * 4 * D].rearrange("p (c e) -> p c e", c=NC)
        wlin = room[:, NC * 4 * D:NC * 5 * D].rearrange("p (c e) -> p c e", c=NC)
        wlin_rest = room[:, NC * 5 * D:NC * 6 * D].rearrange("p (c e) -> p c e", c=NC)

        b_v_rep = room[:, NC * 6 * D:NC * 6 * D + NT * P].rearrange("p (t m) -> p t m", t=NT)

        ps_t = ps("ps_t", [P, 2, S])
        ps_s = ps("ps_s", [P, 2, 2, S])
        ps_o = ps("ps_o", [P, S])
        ps_m = ps("ps_m", [P, S])

        ident_in = sem("ident_in")
        w_in = sem("w_in")
        consts = sem("consts")
        wqkv_ready = sem("wqkv_ready")
        const_v = sem("const_v")
        half_set = sem("half_set")
        bias_done = sem("bias_done")
        ones = sem("ones")
        ks_ones = sem("ks_ones")
        x_in = [sem(f"x_in{i}") for i in range(2)]
        xr_in = sem("xr_in")
        stacked = [[sem(f"stacked{t}{i}") for i in range(2)] for t in range(NT)]
        rows_in = [sem(f"rows_in{t}") for t in range(NT)]
        stored = sem("stored")
        met = sem("met")
        xt_done = sem("xt_done")
        qk_done = sem("qk_done")
        v_done = sem("v_done")
        s_done = sem("s_done")
        mt_done = sem("mt_done")
        st_done = sem("st_done")
        pv_done = sem("pv_done")
        proj_done = sem("proj_done")
        xq_done = sem("xq_done")
        lin_done = sem("lin_done")
        xnT_ready = sem("xnT_ready")
        oT_high = sem("oT_high")
        whole_ready = sem("whole_ready")
        v_ready = sem("v_ready")
        exp_done = sem("exp_done")
        hqT_ready = sem("hqT_ready")
        ln1_sums = sem("ln1_sums")
        ln1_mv = sem("ln1_mv")
        ln1_ready = sem("ln1_ready")
        ln2_sums = sem("ln2_sums")
        ln2_mv = sem("ln2_mv")
        ln2_ready = sem("ln2_ready")
        max_done = sem("max_done")
        nmax_split = sem("nmax_split")
        ot_ready = sem("ot_ready")
        rden_ready = sem("rden_ready")
        on_ready = sem("on_ready")
        oT_ready = sem("oT_ready")
        h_ready = sem("h_ready")
        pow2 = sem("pow2")
        round_c = sem("round_c")
        y_ready = sem("y_ready")
        rs1_ready = sem("rs1_ready")
        xn_ready = sem("xn_ready")
        rest_ready = sem("rest_ready")
        part2 = sem("part2")
        xnT_low = sem("xnT_low")
        oT_low = sem("oT_low")
        part3 = sem("part3")
        res_ready = sem("res_ready")
        rs2_pow = sem("rs2_pow")
        rs2_ready = sem("rs2_ready")
        hn_ready = sem("hn_ready")
        hb_ready = sem("hb_ready")
        clipped = sem("clipped")
        sum_c = sem("sum_c")
        hq_ready = sem("hq_ready")

        def past(count):
            return not isinstance(count, int) or count > 0

        def run_slots(eng, slot, finish, prepare=None):
            def present(u):
                return lambda behind: 0 <= u - behind < B
            for u in range(LOOP_FROM):
                slot(u, u % 2, present(u))
                if u == 0 and prepare:
                    prepare()
            with eng.Fori(0, (LOOP_TO - LOOP_FROM) // 2) as i:
                for half in range(2):
                    slot(i * 2 + (LOOP_FROM + half), half, lambda behind: True)
            for u in range(LOOP_TO, NSLOT - 1):
                slot(u, u % 2, present(u))
            finish(B - 1)

        block = ctx.enter_context(nc.Block())

        @block.sync
        def _(sp):
            sp.dma_start(xin[0][:], x_d[0]).then_inc(x_in[0], 16)
            sp.dma_start(ident[:], eye).then_inc(ident_in, 16)
            sp.dma_start(b_qk[:], qk_bT).then_inc(ident_in, 16)
            sp.dma_start(wqkv, qkv_wT.rearrange("(c p) e -> p c e", p=P)).then_inc(w_in, 16)
            for dst, src in ((wproj, proj_wT.rearrange("(c p) e -> p c e", p=P)), (b_v[:], v_bT),
                             (wlin, lin_wT.rearrange("(c p) e -> p c e", p=P)),
                             (b_proj[:], proj_b.partition_broadcast(P)),
                             (b_lin[:], lin_b.partition_broadcast(P)),
                             (s_in[:], in_scale.partition_broadcast(P)),
                             (s_w[:], w_scale.partition_broadcast(P))):
                sp.dma_start(dst, src).then_inc(consts, 16)
            sp.wait_ge(ones, 1)
            for par in range(2):
                for t in range(NT):
                    for i in range(3):
                        sp.dma_start(ks[par][KR + i:KR + i + 1, HT * t:HT * (t + 1), :],
                                     nmax[:, t, i, :]).then_inc(ks_ones, 16)

            def settled():
                sp.sem_inc(met, 1)

            def load(b, par):
                if past(b - 1):
                    sp.wait_ge(xn_ready, b - 1)
                settled()
                sp.dma_start(xin[par][:], x_d[bass.ds(b, 1)].rearrange("a p j d -> (a p) j d")).then_inc(x_in[par], 16)

            def reload(b, par):
                if past(b):
                    sp.wait_ge(hq_ready, b)
                settled()
                sp.dma_start(xres[:], x_d[bass.ds(b, 1)].rearrange("a p j d -> (a p) j d")).then_inc(xr_in, 16)

            def stack(b, par, t):
                sp.wait_ge(part3, 4 * b + 2 * t + 2)
                settled()
                if past(2 * STEPS * (b - 2) + (t + 1) * STEPS):
                    sp.wait_ge(st_done, 2 * STEPS * (b - 2) + (t + 1) * STEPS)
                settled()
                for r, (pq, pk) in enumerate(zip(Q_PARTS, K_PARTS)):
                    rows = slice(HD * r, HD * (r + 1))
                    for dst, src in ((qs, parts[:, 2 * t, pq, :]), (ks, parts[:, 2 * t + 1, pk, :])):
                        sp.dma_start(dst[par][rows, HT * t:HT * (t + 1), :], src).then_inc(stacked[t][par], 16)

            def rows(b, par, t):
                sp.wait_ge(nmax_split, 8 * b + 4 * t + 4)
                settled()
                for i in range(3):
                    sp.dma_start(qs[par][KR + i:KR + i + 1, HT * t:HT * (t + 1), :],
                                 nmax[:, t, i, :]).then_inc(rows_in[t], 16)

            def store(b, par):
                sp.wait_ge(y_ready, 2 * b + 2)
                settled()
                sp.dma_start(out_d[bass.ds(b, 1)].rearrange("a p j d -> (a p) j d"), h[:]).then_inc(stored, 16)

            def slot(u, par, present):
                if present(-1):
                    load(u + 1, 1 - par)
                if present(2):
                    rows(u - 2, par, 1)
                if present(0):
                    stack(u, par, 0)
                if present(1):
                    rows(u - 1, 1 - par, 0)
                if present(2):
                    reload(u - 2, par)
                if present(3):
                    store(u - 3, 1 - par)
                if present(0):
                    stack(u, par, 1)

            def finish(b):
                for half in range(2):
                    sp.wait_ge(y_ready, 2 * b + half + 1)
                    sp.dma_start(out_d[b, :, 2 * half:2 * half + 2, :], h[:, 2 * half:2 * half + 2, :]).then_inc(stored, 16)

            run_slots(sp, slot, finish)
            sp.wait_ge(stored, 16 * (B + 1))

        @block.tensor
        def _(pe):
            bank_user = [None, 0, 0]

            def take_bank(u, name, n, behind):
                last, m, b = bank_user[0], bank_user[1], u - bank_user[2]
                if last in ("transpose_x", "project_qk", "project_v"):
                    reader, value = {"transpose_x": (xnT_ready, 2 * b), "project_qk": (whole_ready, 4 * b),
                                     "project_v": (v_ready, 2 * b)}[last]
                    pe.wait_ge(reader, value + m + 1)
                elif last == "transpose_max":
                    pe.wait_ge(nmax_split, 8 * b + 4 * m + 2)
                elif last == "project_out":
                    pe.wait_ge(h_ready, 2 * b + m + 1)
                elif last == "transpose_hq":
                    pe.wait_ge(hqT_ready, b + 1)
                elif last == "linear":
                    pe.wait_ge(y_ready, 2 * b + m + 1)
                elif last == "bias":
                    pe.wait_ge(const_v, 4)
                bank_user[:] = [name, n, behind]

            def transpose_x(u, c):
                first = isinstance(u, int) and u == 0
                bank = ps_t[:, c, :] if first else ps_m[:]
                if not first:
                    take_bank(u, "transpose_x", c, 0)
                pe.wait_ge(xn_ready, u + 1)
                for j in range(NJ):
                    last = nc.tensor.transpose(bank[:, j * P:(j + 1) * P], xn[:, j, c * P:(c + 1) * P], ident[:])
                last.then_inc(xt_done, 1)

            def project_qk(u, n):
                start = isinstance(u, int) and u == 0
                bank = ps_s[:, n // 2, n % 2, :] if start else ps_m[:]
                if not start:
                    take_bank(u, "project_qk", n, 0)
                if n == 0:
                    pe.wait_ge(xnT_low, 2 * u + 2)
                    if start:
                        pe.wait_ge(wqkv_ready, 2)
                first = (n % 2) * D + (n // 2) * P
                for m, (pw, px) in enumerate(PAIRS):
                    for c in range(NC):
                        last = nc.tensor.matmul(bank, wqkv_p[:, pw, c, first:first + P], xnT_p[:, px, c, :],
                                                start=(m == 0 and c == 0), stop=(m == 2 and c == NC - 1))
                last.then_inc(qk_done, 1)

            def project_v(u, half):
                take_bank(u, "project_v", half, 1)
                for j in range(2):
                    tok = slice((2 * half + j) * P, (2 * half + j + 1) * P)
                    for m, (pw, px) in enumerate(PAIRS):
                        for c in range(NC):
                            last = nc.tensor.matmul(ps_m[:, j * D:(j + 1) * D], xnT_p[:, px, c, tok],
                                                    wqkv_p[:, pw, c, 2 * D:3 * D],
                                                    start=(m == 0 and c == 0), stop=(m == 2 and c == NC - 1))
                last.then_inc(v_done, 1)

            def transpose_max(u, t, behind):
                take_bank(u, "transpose_max", t, behind)
                pe.wait_ge(max_done, STEPS * (u - behind) + (t + 1) * STEPS // 2)
                nc.tensor.transpose(ps_m[0:HT * NJ, 0:P], mx[:, t, :], ident[:]).then_inc(mt_done, 1)

            def project_out(u, half, bank=None):
                if bank is None:
                    take_bank(u, "project_out", half, 3)
                    bank = ps_m[:]
                if isinstance(u, int) and u == 3:
                    pe.wait_ge(const_v, 9)
                if half == 0:
                    pe.wait_ge(oT_low, NT * (u - 3) + NT)
                for j in range(2):
                    tok = slice((2 * half + j) * P, (2 * half + j + 1) * P)
                    for m, (pw, px) in enumerate(PAIRS):
                        for t in range(NT):
                            last = nc.tensor.matmul(bank[:, j * D:(j + 1) * D], oT_p[:, px, t, tok],
                                                    wproj_p[:, pw, t, :],
                                                    start=(m == 0 and t == 0), stop=(m == 2 and t == NT - 1))
                last.then_inc(proj_done, 1)

            def transpose_hq(u):
                take_bank(u, "transpose_hq", 0, 3)
                if isinstance(u, int) and u == 3:
                    pe.wait_ge(const_v, 9)
                pe.wait_ge(hq_ready, u - 3 + 1)
                psb = ps_m[:].bitcast(BF16)
                for c in range(NC):
                    for j in range(NJ):
                        last = nc.tensor.transpose(psb[:, c * S + j * P:c * S + (j + 1) * P],
                                                   hq[:, j, c * P:(c + 1) * P], ident_b[:])
                last.then_inc(xq_done, 1)

            def linear(u, half, bank=None):
                if isinstance(u, int) and u == 3:
                    pe.wait_ge(const_v, 9)
                if bank is None:
                    take_bank(u, "linear", half, 3)
                    bank = ps_m[:]
                    if half == 0:
                        pe.wait_ge(hqT_ready, u - 3 + 1)
                for j in range(2):
                    tok = slice((2 * half + j) * P, (2 * half + j + 1) * P)
                    for c in range(NC):
                        for part in range(2):
                            last = nc.tensor.matmul(bank[:, j * D:(j + 1) * D], hqT[:, c, tok], wlin_p[:, part, c, :],
                                                    start=(c == 0 and part == 0),
                                                    stop=(c == NC - 1 and part == 1))
                last.then_inc(lin_done, 1)

            def scores_t(b, par, s, a):
                n, i = s // 4, s % 4
                t, odd, kp = n // 4, n // 2 % 2, n % 2
                head = HT * t + 2 * i + odd
                if s in (0, STEPS // 2) and a == 0:
                    pe.wait_ge(rows_in[t], 48 * b + 48)
                    if isinstance(b, int) and b == 0:
                        pe.wait_ge(ks_ones, 16 * 12)
                if past(2 * STEPS * b + 2 * s + a - 1):
                    pe.wait_ge(exp_done, 2 * STEPS * b + 2 * s + a - 1)
                keys = slice((2 * kp + a) * P, (2 * kp + a + 1) * P)
                nc.tensor.matmul(ps_t[:, a, :], ks[par][0:KM, head, keys], qs[par][0:KM, head, :],
                                 start=True, stop=True).then_inc(st_done, 1)

            def scores(b, par, s, a):
                head = s // 2
                if s in (0, STEPS // 2) and a == 0:
                    t = s // (STEPS // 2)
                    pe.wait_ge(stacked[t][par], 96 * (b - par) + 192)
                if a == 0 and past(STEPS * b + s - 1):
                    pe.wait_ge(max_done, STEPS * b + s - 1)
                queries = slice((2 * (s % 2) + a) * P, (2 * (s % 2) + a + 1) * P)
                last = nc.tensor.matmul(ps_s[:, s % 2, a, :], qs[par][0:KR, head, queries],
                                        ks[par][0:KR, head, :], start=True, stop=True)
                if a == 1:
                    last.then_inc(s_done, 1)

            def values(b, par, n, a):
                t, odd, kp = n // 4, n // 2 % 2, n % 2
                if a == 0:
                    if n == 0:
                        pe.wait_ge(v_ready, 2 * b + 2)
                    pe.wait_ge(exp_done, 2 * (STEPS * b + 4 * n + 4))
                    if kp == 0:
                        if past(4 * b + n // 2):
                            pe.wait_ge(ot_ready, 4 * b + n // 2)
                for i in range(4):
                    head = HT * t + 2 * i + odd
                    last = nc.tensor.matmul(ps_o[32 * i:32 * i + VW, :], vt[par][:, 2 * kp + a, head, :],
                                            pt[n % 2][:, i, a, :], start=(kp == 0 and a == 0),
                                            stop=(kp == 1 and a == 1))
                if a == 1:
                    last.then_inc(pv_done, 1)

            def slot(u, par, present):
                bank_user[2] += 1
                for s in range(STEPS):
                    if present(2):
                        scores_t(u - 2, par, s, 0)
                    if present(1):
                        scores(u - 1, 1 - par, s, 0)
                        if not present(2):
                            scores(u - 1, 1 - par, s, 1)
                    if present(2):
                        scores_t(u - 2, par, s, 1)
                    if s == TRANSPOSE_MAX[1] and present(2):
                        transpose_max(u, 1, 2)
                    if s in PROJECT_V and present(1):
                        project_v(u, PROJECT_V.index(s))
                    if s in PROJECT_OUT and present(3):
                        project_out(u, PROJECT_OUT.index(s))
                    if s in TRANSPOSE_X and present(0):
                        transpose_x(u, TRANSPOSE_X.index(s))
                    if s in PROJECT_QK and present(0):
                        project_qk(u, PROJECT_QK.index(s))
                    if s == TRANSPOSE_MAX[0] and present(1):
                        transpose_max(u, 0, 1)
                    if s == TRANSPOSE_HQ and present(3):
                        transpose_hq(u)
                    if s in LINEAR and present(3):
                        linear(u, LINEAR.index(s))
                    if s % 2:
                        n = s // 4 - 1
                        if n >= 0 and present(2):
                            values(u - 2, par, n, s // 2 % 2)
                        if n < 0 and present(3):
                            values(u - 3, 1 - par, UNITS - 1, s // 2 % 2)
                    if present(1) and present(2):
                        scores(u - 1, 1 - par, s, 1)

            def prepare():
                pe.wait_ge(consts, 16 * 7)
                pe.wait_ge(const_v, 2)
                take_bank(0, "bias", 0, 0)
                for t in range(NT):
                    last = nc.tensor.matmul(ps_m[:, 0:D], b_v_rep[:, t, :], wproj[:, t, :],
                                            start=(t == 0), stop=(t == NT - 1))
                last.then_inc(bias_done, 1)

            def finish(b):
                for a in range(2):
                    values(b, b % 2, UNITS - 1, a)
                for half in range(2):
                    project_out(b + 3, half, ps_s[:, half, 0, :])
                for half in range(2):
                    pe.wait_ge(hq_ready, b + half + 1)
                    psb = ps_t[:, half, :].bitcast(BF16)
                    for c in range(NC):
                        for j in range(2):
                            last = nc.tensor.transpose(psb[:, (2 * c + j) * P:(2 * c + j + 1) * P],
                                                       hq[:, 2 * half + j, c * P:(c + 1) * P], ident_b[:])
                    last.then_inc(xq_done, 1)
                    pe.wait_ge(hqT_ready, b + half + 1)
                    linear(b + 3, half, ps_s[:, half, 1, :])

            pe.wait_ge(ident_in, 32)
            run_slots(pe, slot, finish, prepare)

        @block.scalar
        def _(act):
            def exps(b, s, a):
                n, i = s // 4, s % 4
                if i == 0 and a == 0 and past(UNITS * b + n - 1):
                    act.wait_ge(pv_done, UNITS * b + n - 1)
                if isinstance(b, int) and b == 0 and s == 0:
                    act.wait_ge(const_v, 9)
                act.wait_ge(st_done, 2 * (STEPS * b + s) + a + 1)
                nc.scalar.activation(pt[n % 2][:, i, a, :], ps_t[:, a, :], ACT.Exp, scale=SCALE).then_inc(exp_done, 1)

            def copy_v(b, par, half):
                act.wait_ge(v_done, 2 * b + half + 1)
                if isinstance(b, int) and b == 0:
                    act.wait_ge(ones, 3)
                if past(UNITS * (b - 1)):
                    act.wait_ge(pv_done, UNITS * (b - 1))
                nc.scalar.copy(vt[par][:, 2 * half:2 * half + 2, :, 0:HD],
                               ps_m[:].rearrange("p (j h e) -> p j h e", j=2, h=H)).then_inc(v_ready, 1)

            def copy_xnT(b, c):
                bank = ps_t[:, c, :] if isinstance(b, int) and b == 0 else ps_m[:]
                act.wait_ge(xt_done, 2 * b + c + 1)
                if past(b):
                    act.wait_ge(v_done, 2 * b)
                nc.scalar.copy(xnT_p[:, 0, c, :], bank)
                if past(2 * b + c):
                    act.wait_ge(xnT_low, 2 * b + c)
                nc.scalar.copy(xnT[:], bank).then_inc(xnT_ready, 1)

            def copy_oT(b, t):
                act.wait_ge(oT_ready, NT * b + t + 1)
                if past(b):
                    act.wait_ge(proj_done, 2 * b)
                nc.scalar.copy(oT_p[:, 0, t, :], oT[:]).then_inc(oT_high, 1)

            def copy_qk(b, par, n):
                t, bias = n // 2, b_qk[:, (n % 2) * NT + n // 2:(n % 2) * NT + n // 2 + 1]
                bank = ps_s[:, n // 2, n % 2, :] if isinstance(b, int) and b == 0 else ps_m[:]
                act.wait_ge(qk_done, 4 * b + n + 1)
                if past(b):
                    act.wait_ge(stacked[t][1 - par], 96 * (b - 2 + par) + 192)
                nc.scalar.activation(parts[:, n, 0, :], bank, ACT.Identity, bias=bias)
                if past(4 * b + n - 1):
                    act.wait_ge(part3, 4 * b + n - 1)
                nc.scalar.activation(whole[:, n % 2, :], bank, ACT.Identity, bias=bias).then_inc(whole_ready, 1)

            def copy_hqT(b):
                act.wait_ge(xq_done, b + 1)
                if past(b):
                    act.wait_ge(lin_done, 2 * b)
                nc.scalar.copy(hqT[:].rearrange("p c n -> p (c n)"), ps_m[:].bitcast(BF16)).then_inc(hqT_ready, 1)

            def slot(u, par, present):
                for s in range(STEPS):
                    if present(2):
                        exps(u - 2, s, 0)
                        exps(u - 2, s, 1)
                    if s == COPY_OT[1] and present(3):
                        copy_oT(u - 3, 1)
                    if s == COPY_OT[0] and present(2):
                        copy_oT(u - 2, 0)
                    if s in PROJECT_V and present(1):
                        copy_v(u - 1, 1 - par, PROJECT_V.index(s))
                    if s in TRANSPOSE_X and present(0):
                        copy_xnT(u, TRANSPOSE_X.index(s))
                    if s in PROJECT_QK and present(0):
                        copy_qk(u, par, PROJECT_QK.index(s))
                    if s == TRANSPOSE_HQ and present(3):
                        copy_hqT(u - 3)

            def finish(b):
                copy_oT(b, 1)
                for half in range(2):
                    act.wait_ge(xq_done, b + half + 1)
                    if half == 0:
                        act.wait_ge(lin_done, 2 * b)
                    nc.scalar.copy(hqT[:, :, 2 * half * P:2 * (half + 1) * P],
                                   ps_t[:, half, :].bitcast(BF16)[:, 0:S].rearrange("p (c n) -> p c n", c=NC)
                                   ).then_inc(hqT_ready, 1)

            act.wait_ge(half_set, 1)
            nc.scalar.activation(table[:], half_neg[:, 0:1], ACT.Exp)
            act.wait_ge(ident_in, 32)
            run_slots(act, slot, finish)

        @block.vector
        def _(dve):
            def prepare():
                dve.wait_ge(w_in, 16)
                dve.tensor_copy(wqkv_p[:, 0], wqkv).then_inc(wqkv_ready, 1)
                dve.wait_ge(wqkv_ready, 1)
                dve.tensor_tensor(wqkv_p[:, 1], wqkv, wqkv_p[:, 0].bitcast(F32), ALU.subtract).then_inc(wqkv_ready, 1)

                for c in range(NC):
                    dve.wait_ge(xnT_ready, c + 1)
                    dve.tensor_tensor(xnT_p[:, 1, c, :], xnT[:], xnT_p[:, 0, c, :].bitcast(F32),
                                      ALU.subtract).then_inc(xnT_low, 1)
                for n in range(2 * NT):
                    rest = whole[:, n % 2, :]
                    dve.wait_ge(whole_ready, n + 1)
                    dve.tensor_tensor(rest, rest, parts[:, n, 0, :], ALU.subtract).then_inc(rest_ready, 1)
                    dve.wait_ge(rest_ready, n + 1)
                    dve.tensor_copy(parts[:, n, 1, :], rest).then_inc(part2, 1)
                    dve.wait_ge(part2, n + 1)
                    dve.tensor_tensor(parts[:, n, 2, :], rest, parts[:, n, 1, :], ALU.subtract).then_inc(part3, 1)
                dve.wait_ge(consts, 16 * 7)
                dve.reciprocal(s_inv[:], s_in[:]).then_inc(const_v, 1)
                dve.tensor_copy(b_v_rep, b_v[:].unsqueeze(2).to_broadcast([P, NT, P])).then_inc(const_v, 1)
                dve.tensor_copy(wproj_p[:, 0], wproj).then_inc(const_v, 1)
                dve.wait_ge(bias_done, 1)
                dve.tensor_tensor(b_proj[:], ps_m[:, 0:D], b_proj[:], ALU.add).then_inc(const_v, 1)
                dve.wait_ge(const_v, 3)
                dve.tensor_tensor(wproj_p[:, 1], wproj, wproj_p[:, 0].bitcast(F32), ALU.subtract).then_inc(const_v, 1)
                dve.tensor_copy(ident_b[:], ident[:]).then_inc(const_v, 1)
                dve.tensor_scalar(wlin_rest, wlin, s_w[:, 0:1], None, ALU.mult).then_inc(const_v, 1)
                dve.wait_ge(const_v, 7)
                dve.tensor_copy(wlin_p[:, 0], wlin_rest).then_inc(const_v, 1)
                dve.wait_ge(const_v, 8)
                dve.tensor_tensor(wlin_p[:, 1], wlin_rest, wlin_p[:, 0].bitcast(F32), ALU.subtract).then_inc(const_v, 1)

            def maxima(b, s):
                t = s // (STEPS // 2)
                if s in (0, STEPS // 2) and past(NT * (b - 1) + t + 1):
                    dve.wait_ge(mt_done, NT * (b - 1) + t + 1)
                dve.wait_ge(s_done, STEPS * b + s + 1)
                col = 2 * (s % (STEPS // 2))
                dve.tensor_reduce(mx[:, t, col:col + 2], ps_s[:, s % 2, :, :], AX_X, ALU.max).then_inc(max_done, 1)

            def ln1_sum(b, par, j):
                if j == 0:
                    dve.wait_ge(x_in[par], 8 * (b - par) + 16)
                    if past(b):
                        dve.wait_ge(xn_ready, b)
                dve.bn_stats(st1[:, j, :], xin[par][:, j, :]).then_inc(ln1_sums, 1)

            def ln1_finish(b):
                dve.wait_ge(ln1_sums, NJ * b + NJ)
                dve.sem_inc(met, 1)
                for j in range(NJ):
                    last = dve.bn_aggr(mv1[:, j, :], st1[:, j, :])
                last.then_inc(ln1_mv, 1)
                dve.wait_ge(ln1_mv, b + 1)
                dve.tensor_scalar(nm1[:], mv1[:, :, 0], -1.0, None, ALU.mult).then_inc(ln1_ready, 1)
                dve.tensor_scalar(ve1[:], mv1[:, :, 1], EPS, None, ALU.add).then_inc(ln1_ready, 1)

            def ln2_sum(b, j):
                if j == 0 and past(b):
                    dve.wait_ge(hn_ready, b)
                if j % 2 == 0:
                    dve.wait_ge(h_ready, 2 * b + j // 2 + 1)
                    dve.sem_inc(met, 1)
                dve.bn_stats(st2[:, j, :], h[:, j, :]).then_inc(ln2_sums, 1)

            def ln2_finish(b):
                dve.wait_ge(ln2_sums, NJ * b + NJ)
                dve.sem_inc(met, 1)
                for j in range(NJ):
                    last = dve.bn_aggr(mv2[:, j, :], st2[:, j, :])
                last.then_inc(ln2_mv, 1)
                dve.wait_ge(ln2_mv, b + 1)
                dve.tensor_scalar(nm2[:], mv2[:, :, 0], -1.0, None, ALU.mult).then_inc(ln2_ready, 1)
                dve.tensor_scalar(ve2[:], mv2[:, :, 1], EPS, None, ALU.add).then_inc(ln2_ready, 1)

            def split_max(b, t):
                dve.wait_ge(mt_done, NT * b + t + 1)
                if past(b):
                    dve.wait_ge(rows_in[t], 48 * b)
                elif t == 0:
                    dve.wait_ge(ks_ones, 16 * 12)
                mT = ps_m[0:HT * NJ, 0:P]
                dve.tensor_scalar(nmax[:, t, 0, :], mT, -1.0, None, ALU.mult).then_inc(nmax_split, 1)
                dve.wait_ge(nmax_split, 8 * b + 4 * t + 1)
                dve.scalar_tensor_tensor(out=nmax_r[:], in0=mT, scalar=-1.0, in1=nmax[:, t, 0, :],
                                         op0=ALU.mult, op1=ALU.subtract).then_inc(nmax_split, 1)
                dve.wait_ge(nmax_split, 8 * b + 4 * t + 2)
                dve.tensor_copy(nmax[:, t, 1, :], nmax_r[:]).then_inc(nmax_split, 1)
                dve.wait_ge(nmax_split, 8 * b + 4 * t + 3)
                dve.tensor_tensor(nmax[:, t, 2, :], nmax_r[:], nmax[:, t, 1, :], ALU.subtract).then_inc(nmax_split, 1)

            def out_blocks(b, g):
                dve.wait_ge(pv_done, UNITS * b + 2 * g + 2)
                if past(4 * b + g):
                    dve.wait_ge(on_ready, 4 * b + g)
                dve.transpose(ot[:].rearrange("p a c -> p (a c)"), ps_o[:]).then_inc(ot_ready, 1)

            def out_reciprocal(b, g):
                dve.wait_ge(ot_ready, 4 * b + g + 1)
                dve.reciprocal(rden[:], ot[:, :, HD]).then_inc(rden_ready, 1)

            def out_back(b, t):
                dve.wait_ge(on_ready, 4 * b + 2 * t + 2)
                if past(NT * b + t):
                    dve.wait_ge(oT_low, NT * b + t)
                dve.transpose(oT[:], on[:].rearrange("p a c -> p (a c)")).then_inc(oT_ready, 1)

            def add_residual(b, half, bank=ps_m[:]):
                dve.wait_ge(proj_done, 2 * b + half + 1)
                if half == 0:
                    dve.wait_ge(res_ready, b + 1)
                    if past(b):
                        dve.wait_ge(stored, 16 * b)
                tok = slice(2 * half, 2 * half + 2)
                dve.tensor_tensor(h[:, tok, :].rearrange("p j d -> p (j d)"), bank,
                                  xres[:, tok, :].rearrange("p j d -> p (j d)"), ALU.add).then_inc(h_ready, 1)

            def power_of_two(b):
                dve.wait_ge(clipped, b + 1)
                dve.tensor_scalar(cr[:].bitcast(U32), hn[:].bitcast(U32), EXPONENT, None,
                                  ALU.bitwise_and).then_inc(pow2, 1)

            def rounding_constant(b):
                dve.wait_ge(pow2, b + 1)
                dve.tensor_scalar(cr[:], cr[:], FP8_MIN_NORMAL, FP8_ROUND, ALU.max, ALU.mult).then_inc(round_c, 1)

            def finish_linear(b, half, bank=ps_m[:], halves=False):
                dve.wait_ge(lin_done, 2 * b + half + 1)
                if half == 0 or halves:
                    dve.wait_ge(hb_ready, b + half + 1)
                tok = slice(2 * half, 2 * half + 2)
                dve.scalar_tensor_tensor(out=h[:, tok, :].rearrange("p j d -> p (j d)"), in0=bank,
                                         scalar=s_in[:, 0:1], in1=h[:, tok, :].rearrange("p j d -> p (j d)"),
                                         op0=ALU.mult, op1=ALU.add).then_inc(y_ready, 1)

            def slot(u, par, present):
                for s in range(STEPS):
                    if present(3):
                        if s == OUT_BLOCKS[3]:
                            out_blocks(u - 3, 3)
                        if s in PROJECT_OUT:
                            add_residual(u - 3, PROJECT_OUT.index(s))
                        if s in LINEAR:
                            finish_linear(u - 3, LINEAR.index(s))
                    if s == TRANSPOSE_MAX[1] and present(2):
                        split_max(u - 2, 1)
                    if s in OUT_BLOCKS[:3] and present(2):
                        out_blocks(u - 2, OUT_BLOCKS.index(s))
                    if s == TRANSPOSE_MAX[0] and present(1):
                        split_max(u - 1, 0)

                    if present(1):
                        maxima(u - 1, s)

                    if present(3):
                        if s == OUT_BLOCKS[3]:
                            out_reciprocal(u - 3, 3)
                        if s == OUT_BACK[1]:
                            out_back(u - 3, 1)
                        for j in range(NJ):
                            if s == LN2_SUM[j]:
                                ln2_sum(u - 3, j)
                        if s == LN2_END:
                            ln2_finish(u - 3)
                        if s == POWER_OF_TWO:
                            power_of_two(u - 3)
                        if s == ROUNDING_CONSTANT:
                            rounding_constant(u - 3)
                    if present(-1):
                        if s in LN1_SUM:
                            ln1_sum(u + 1, 1 - par, LN1_SUM.index(s))
                        if s == LN1_END:
                            ln1_finish(u + 1)
                    if present(2):
                        if s in OUT_BLOCKS[:3]:
                            out_reciprocal(u - 2, OUT_BLOCKS.index(s))
                        if s == OUT_BACK[0]:
                            out_back(u - 2, 0)

            def finish(b):
                out_blocks(b, 3)
                out_reciprocal(b, 3)
                dve.wait_ge(rden_ready, 4 * b + 4)
                dve.tensor_tensor(on[:, :, HD:2 * HD], ot[:, :, 0:HD],
                                  rden[:].unsqueeze(2).to_broadcast([P, S // 32, HD]), ALU.mult).then_inc(on_ready, 1)
                out_back(b, 1)
                dve.wait_ge(oT_high, NT * b + 2)
                dve.tensor_tensor(oT_p[:, 1, 1, :], oT[:], oT_p[:, 0, 1, :].bitcast(F32),
                                  ALU.subtract).then_inc(oT_low, 1)
                for half in range(2):
                    tok = slice(2 * half, 2 * half + 2)
                    add_residual(b, half, ps_s[:, half, 0, :])
                    for j in range(2):
                        ln2_sum(b, 2 * half + j)
                    dve.wait_ge(ln2_sums, NJ * b + 2 * half + 2)
                    for j in range(2 * half, 2 * half + 2):
                        last = dve.bn_aggr(mv2[:, j, :], st2[:, j, :])
                    last.then_inc(ln2_mv, 1)
                    dve.wait_ge(ln2_mv, b + half + 1)
                    dve.tensor_scalar(nm2[:, tok], mv2[:, tok, 0], -1.0, None, ALU.mult).then_inc(ln2_ready, 1)
                    dve.tensor_scalar(ve2[:, tok], mv2[:, tok, 1], EPS, None, ALU.add).then_inc(ln2_ready, 1)
                for half in range(2):
                    tok = slice(2 * half, 2 * half + 2)
                    dve.wait_ge(rs2_ready, b + half + 1)
                    for j in range(2 * half, 2 * half + 2):
                        last = dve.tensor_scalar(hn[:, j, :], h[:, j, :], nm2[:, j:j + 1], rs2[:, j:j + 1],
                                                 ALU.add, ALU.mult)
                    last.then_inc(hn_ready, 1)
                    dve.wait_ge(hn_ready, b + half + 1)
                    dve.tensor_scalar(hn[:, tok], hn[:, tok], FP8_MAX, -FP8_MAX, ALU.min, ALU.max).then_inc(clipped, 1)
                    dve.wait_ge(clipped, b + half + 1)
                    dve.tensor_scalar(cr[:, tok].bitcast(U32), hn[:, tok].bitcast(U32), EXPONENT, None,
                                      ALU.bitwise_and).then_inc(pow2, 1)
                    dve.wait_ge(pow2, b + half + 1)
                    dve.tensor_scalar(cr[:, tok], cr[:, tok], FP8_MIN_NORMAL, FP8_ROUND, ALU.max,
                                      ALU.mult).then_inc(round_c, 1)
                    dve.wait_ge(round_c, b + half + 1)
                    dve.tensor_tensor(hn[:, tok], hn[:, tok], cr[:, tok], ALU.add).then_inc(sum_c, 1)
                    dve.wait_ge(sum_c, b + half + 1)
                    dve.tensor_tensor(hq[:, tok], hn[:, tok], cr[:, tok], ALU.subtract).then_inc(hq_ready, 1)
                for half in range(2):
                    finish_linear(b, half, ps_s[:, half, 1, :], halves=True)

            dve.memset(half_neg[:], -0.5).then_inc(half_set, 1)
            for j in range(NJ):
                ln1_sum(0, 0, j)
            ln1_finish(0)
            prepare()
            run_slots(dve, slot, finish)

        @block.gpsimd
        def _(pool):
            def settled():
                pool.sem_inc(met, 1)

            def layernorm_x(b, par):
                pool.wait_ge(ln1_ready, 2 * b + 2)
                pool.tensor_tensor(rs1[:], ve1[:], half_neg[:], ALU.pow).then_inc(rs1_ready, 1)
                pool.wait_ge(rs1_ready, b + 1)
                if past(b):
                    pool.wait_ge(xt_done, 2 * b)
                settled()
                for j in range(NJ):
                    last = pool.tensor_scalar(xn[:, j, :], xin[par][:, j, :], nm1[:, j:j + 1], rs1[:, j:j + 1],
                                              ALU.add, ALU.mult)
                last.then_inc(xn_ready, 1)

            def low_xnT(b, c):
                pool.wait_ge(xnT_ready, 2 * b + c + 1)
                if past(b):
                    pool.wait_ge(v_done, 2 * b)
                pool.tensor_tensor(xnT_p[:, 1, c, :], xnT[:], xnT_p[:, 0, c, :].bitcast(F32),
                                   ALU.subtract).then_inc(xnT_low, 1)

            def low_oT(b, t):
                pool.wait_ge(oT_high, NT * b + t + 1)
                if past(b):
                    pool.wait_ge(proj_done, 2 * b)
                pool.tensor_tensor(oT_p[:, 1, t, :], oT[:], oT_p[:, 0, t, :].bitcast(F32),
                                   ALU.subtract).then_inc(oT_low, 1)

            def add_bias(b):
                pool.wait_ge(xr_in, 16 * b + 16)
                if isinstance(b, int) and b == 0:
                    pool.wait_ge(const_v, 9)
                pool.tensor_tensor(xres[:], xres[:], b_proj[:].unsqueeze(1).to_broadcast([P, NJ, D]),
                                   ALU.add).then_inc(res_ready, 1)

            def split(b, par, n):
                pool.wait_ge(whole_ready, 4 * b + n + 1)
                pool.tensor_tensor(whole[:, n % 2, :], whole[:, n % 2, :], parts[:, n, 0, :],
                                   ALU.subtract).then_inc(rest_ready, 1)
                pool.wait_ge(rest_ready, 4 * b + n + 1)
                if past(b):
                    pool.wait_ge(stacked[n // 2][1 - par], 96 * (b - 2 + par) + 192)
                settled()
                pool.tensor_scalar(parts[:, n, 1, :], whole[:, n % 2, :], 1.0, 0.0, ALU.mult,
                                   ALU.add).then_inc(part2, 1)
                pool.wait_ge(part2, 4 * b + n + 1)
                pool.tensor_tensor(parts[:, n, 2, :], whole[:, n % 2, :], parts[:, n, 1, :],
                                   ALU.subtract).then_inc(part3, 1)

            def out_divide(b, g):
                pool.wait_ge(rden_ready, 4 * b + g + 1)
                if g % 2 == 0 and past(NT * b + g // 2):
                    pool.wait_ge(oT_ready, NT * b + g // 2)
                half = slice(HD * (g % 2), HD * (g % 2) + HD)
                pool.tensor_tensor(on[:, :, half], ot[:, :, 0:HD], rden[:].unsqueeze(2).to_broadcast([P, S // 32, HD]),
                                   ALU.mult).then_inc(on_ready, 1)

            def layernorm_h(b):
                pool.wait_ge(ln2_ready, 2 * b + 2)
                pool.tensor_tensor(rs2[:], ve2[:], half_neg[:], ALU.pow).then_inc(rs2_pow, 1)
                pool.wait_ge(rs2_pow, b + 1)
                settled()
                pool.tensor_scalar(rs2[:], rs2[:], s_inv[:, 0:1], 0.0, ALU.mult, ALU.add).then_inc(rs2_ready, 1)
                pool.wait_ge(rs2_ready, b + 1)
                settled()
                for j in range(NJ):
                    last = pool.tensor_scalar(hn[:, j, :], h[:, j, :], nm2[:, j:j + 1], rs2[:, j:j + 1],
                                              ALU.add, ALU.mult)
                last.then_inc(hn_ready, 1)
                pool.wait_ge(hn_ready, b + 1)
                settled()
                pool.tensor_scalar(hn[:], hn[:], FP8_MAX, -FP8_MAX, ALU.min, ALU.max).then_inc(clipped, 1)

            def add_linear_bias(b):
                pool.wait_ge(hn_ready, b + 1)
                pool.tensor_tensor(h[:], h[:], b_lin[:].unsqueeze(1).to_broadcast([P, NJ, D]),
                                   ALU.add).then_inc(hb_ready, 1)

            def round_fp8(b):
                pool.wait_ge(round_c, b + 1)
                pool.tensor_tensor(hn[:], hn[:], cr[:], ALU.add).then_inc(sum_c, 1)
                pool.wait_ge(sum_c, b + 1)
                if past(b):
                    pool.wait_ge(xq_done, b)
                pool.tensor_tensor(hq[:], hn[:], cr[:], ALU.subtract).then_inc(hq_ready, 1)

            def slot(u, par, present):
                later = not isinstance(u, int) or u > 0
                if present(0):
                    layernorm_x(u, par)
                if present(3):
                    out_divide(u - 3, 3)
                    low_oT(u - 3, 1)
                if present(0) and later:
                    low_xnT(u, 0)
                if present(2):
                    out_divide(u - 2, 0)
                if present(0) and later:
                    low_xnT(u, 1)
                if present(3):
                    layernorm_h(u - 3)
                if present(0) and later:
                    split(u, par, 0)
                    split(u, par, 1)
                if present(2):
                    out_divide(u - 2, 1)
                if present(3):
                    round_fp8(u - 3)
                    add_linear_bias(u - 3)
                if present(0) and later:
                    split(u, par, 2)
                if present(2):
                    low_oT(u - 2, 0)
                if present(0) and later:
                    split(u, par, 3)
                if present(2):
                    out_divide(u - 2, 2)
                    add_bias(u - 2)

            def prepare():
                pool.memset(vt[0][:], 1.0).then_inc(ones, 1)
                pool.memset(vt[1][:], 1.0).then_inc(ones, 1)
                pool.wait_ge(part3, 4)

            def finish(b):
                for half in range(2):
                    tok = slice(2 * half, 2 * half + 2)
                    pool.wait_ge(ln2_ready, 2 * b + 2 * half + 2)
                    pool.tensor_tensor(rs2[:, tok], ve2[:, tok], half_neg[:, tok], ALU.pow).then_inc(rs2_pow, 1)
                    pool.wait_ge(rs2_pow, b + half + 1)
                    pool.tensor_scalar(rs2[:, tok], rs2[:, tok], s_inv[:, 0:1], 0.0, ALU.mult,
                                       ALU.add).then_inc(rs2_ready, 1)
                for half in range(2):
                    tok = slice(2 * half, 2 * half + 2)
                    pool.wait_ge(hn_ready, b + half + 1)
                    pool.tensor_tensor(h[:, tok], h[:, tok], b_lin[:].unsqueeze(1).to_broadcast([P, 2, D]),
                                       ALU.add).then_inc(hb_ready, 1)

            pool.memset(nmax[:], 1.0).then_inc(ones, 1)
            pool.wait_ge(half_set, 1)
            run_slots(pool, slot, finish, prepare)


def kernel(L0_attn_x, L0_attn_qkv_w, L0_attn_qkv_b, L0_attn_proj_w, L0_attn_proj_b,
           L0_ffn_weight_fp8, L0_ffn_bias, L0_ffn_input_scale, L0_ffn_weight_scale):
    import numpy as np
    import concourse.bacc as bacc
    from concourse.bass_utils import run_bass_kernel_spmd

    order = np.arange(2 * D).reshape(2 * NT, HT, HD).transpose(0, 2, 1).reshape(-1)
    order = np.concatenate([order, np.arange(2 * D, 3 * D)])
    a = {k: np.asarray(v) for k, v in dict(
        x=L0_attn_x, qkv_wT=np.asarray(L0_attn_qkv_w)[order].T,
        qk_bT=np.asarray(L0_attn_qkv_b)[order[:2 * D]].reshape(2 * NT, P).T,
        v_bT=np.asarray(L0_attn_qkv_b)[2 * D:].reshape(NT, P).T,
        proj_wT=np.asarray(L0_attn_proj_w).T, proj_b=L0_attn_proj_b,
        lin_wT=np.asarray(L0_ffn_weight_fp8).T, lin_b=L0_ffn_bias,
        in_scale=L0_ffn_input_scale, w_scale=L0_ffn_weight_scale,
        eye=np.eye(P, dtype=np.float32)).items()}
    nc = bacc.Bacc("TRN2", target_bir_lowering=False, num_devices=1)
    arrays = {f"in_{k}": np.ascontiguousarray(v) for k, v in a.items()}
    args = [nc.dram_tensor(k, v.shape, mybir.dt.from_np(v.dtype), kind="ExternalInput").ap()
            for k, v in arrays.items()]
    out = nc.dram_tensor("out_0", (B, S, D), F32, kind="ExternalOutput").ap()
    block_kernel(nc, *args, out)
    r = run_bass_kernel_spmd(nc, [arrays], core_ids=[0])
    return r.results[0]["out_0"]
```
